# Optimizing a Trainium2 kernel written in Bass

```python
import numpy as np
import jax
import jax.numpy as jnp

def _softmax(x, axis=-1):
    return jax.nn.softmax(x, axis=axis)

def _gelu(x):
    return jax.nn.gelu(x, approximate=True)

def _silu(x):
    return jax.nn.silu(x)

def _sigmoid(x):
    return jax.nn.sigmoid(x)

def _layernorm(x, axis=-1, eps=1e-05):
    m = jnp.mean(x, axis=axis, keepdims=True)
    v = jnp.var(x, axis=axis, keepdims=True)
    return (x - m) / jnp.sqrt(v + eps)

def _scatter_add(tgt, idx, src, axis=0):
    return tgt.at[idx].add(src)

def _segment_sum(src, seg, n):
    return jax.ops.segment_sum(src, seg, n)
kernel_name = 'mk_xattn_seq_d4_seqx_r8_e28e34'

def setup_inputs(seed: int=0):
    np.random.seed(seed)
    _w = jnp.asarray

    def _rec_inputs():
        import jax
        import jax.numpy as jnp
        _rk = jax.random.key(seed)
        x = -0.0002928 + 1 * jax.random.normal(jax.random.fold_in(_rk, 1), (128, 64, 128), jnp.float32)
        _lenS = 64 - jax.random.randint(jax.random.fold_in(_rk, 7), (128,), 0, max(1, 64 // 4) + 1, jnp.int32)
        _lenS2 = 64 - jax.random.randint(jax.random.fold_in(_rk, 8), (128,), 0, max(1, 64 // 4) + 1, jnp.int32)
        _ctx_1024P = jax.random.normal(jax.random.fold_in(_rk, 11), (128, 16, 128), jnp.float32)
        _ctx_1024c = jax.random.dirichlet(jax.random.fold_in(_rk, 511), 0.3 * jnp.ones((16,), jnp.float32), (128, 64))
        _ctx_1024t = jnp.einsum('bsk,bkd->bsd', _ctx_1024c, _ctx_1024P)
        _ctx_1024t = _ctx_1024t * jax.lax.rsqrt(jnp.mean(jnp.square(_ctx_1024t)) + 1e-12) * 0.953939
        ctx_1024 = -1.39393e-06 + 0.999914 * (_ctx_1024t + 0.3 * jax.random.normal(jax.random.fold_in(_rk, 611), (128, 64, 128), jnp.float32))
        return (x, ctx_1024)
    x, ctx_1024 = _rec_inputs()

    def _L0_xattn_setup():
        import jax, jax.numpy as jnp
        import numpy as np
        D_MODEL = 128
        N_HEADS = 16
        D_K = D_MODEL // N_HEADS
        D_FF = 512
        B, S = (2, 256)
        LN_EPS = 1e-05
        NEG_INF = -1e+30

        def layer_norm(x, g, b):
            mu = jnp.mean(x, axis=-1, keepdims=True)
            var = jnp.mean(jnp.square(x - mu), axis=-1, keepdims=True)
            return (x - mu) * jax.lax.rsqrt(var + LN_EPS) * g + b
        key = jax.random.key(seed)
        ks = jax.random.split(key, 16)
        sd = 0.02
        inp = {'query': jax.random.normal(ks[0], (B, S, D_MODEL), jnp.float32), 'key': jax.random.normal(ks[1], (B, S, D_MODEL), jnp.float32), 'values': jax.random.normal(ks[2], (B, S, D_MODEL), jnp.float32), 'Wq': jax.random.normal(ks[3], (D_MODEL, D_MODEL), jnp.float32) * sd, 'bq': jnp.zeros((D_MODEL,), jnp.float32), 'Wk': jax.random.normal(ks[4], (D_MODEL, D_MODEL), jnp.float32) * sd, 'bk': jnp.zeros((D_MODEL,), jnp.float32), 'Wv': jax.random.normal(ks[5], (D_MODEL, D_MODEL), jnp.float32) * sd, 'bv': jnp.zeros((D_MODEL,), jnp.float32), 'Wo': jax.random.normal(ks[6], (D_MODEL, D_MODEL), jnp.float32) * sd, 'bo': jnp.zeros((D_MODEL,), jnp.float32), 'ln1_g': jnp.ones((D_MODEL,), jnp.float32), 'ln1_b': jnp.zeros((D_MODEL,), jnp.float32), 'W1': jax.random.normal(ks[7], (D_MODEL, D_FF), jnp.float32) * sd, 'b1': jnp.zeros((D_FF,), jnp.float32), 'W2': jax.random.normal(ks[8], (D_FF, D_MODEL), jnp.float32) * sd, 'b2': jnp.zeros((D_MODEL,), jnp.float32), 'ln2_g': jnp.ones((D_MODEL,), jnp.float32), 'ln2_b': jnp.zeros((D_MODEL,), jnp.float32), 'mask': 0}
        return inp
    _L0_xattn_all = _L0_xattn_setup()
    _L0_xattn_in = {k: v for k, v in _L0_xattn_all.items() if k in ('Wq', 'bq', 'Wk', 'bk', 'Wv', 'bv', 'Wo', 'bo', 'ln1_g', 'ln1_b', 'W1', 'b1', 'W2', 'b2', 'ln2_g', 'ln2_b')}
    del _L0_xattn_all

    def _L1_xattn_setup():
        import jax, jax.numpy as jnp
        import numpy as np
        DIM = 128
        NUM_HEADS = 16
        HEAD_DIM = DIM // NUM_HEADS
        FF = 4 * DIM
        B, T, S = (8, 64, 512)

        def _perceiver_layer(x, inp, Wq, bq, Wk, bk, Wv, bv, Wo, bo, W1, b1, W2, b2):
            b, t, _ = x.shape
            s = inp.shape[1]
            q = (x @ Wq + bq).reshape(b, t, NUM_HEADS, HEAD_DIM)
            k = (inp @ Wk + bk).reshape(b, s, NUM_HEADS, HEAD_DIM)
            v = (inp @ Wv + bv).reshape(b, s, NUM_HEADS, HEAD_DIM)
            attn = jnp.einsum('bthd,bshd->bhts', q, k)
            attn = jax.nn.softmax(attn / jnp.sqrt(jnp.float32(HEAD_DIM)), axis=-1)
            out = jnp.einsum('bhts,bshd->bthd', attn, v).reshape(b, t, DIM)
            attn_out = out @ Wo + bo
            x = x + attn_out
            h = jax.nn.gelu(x @ W1 + b1, approximate=True)
            x = x + (h @ W2 + b2)
            return x
        key = jax.random.key(seed)
        ks = jax.random.split(key, 14)
        sc = 1.0 / np.sqrt(DIM)
        inp = {'x': jax.random.normal(ks[0], (B, T, DIM), jnp.float32), 'inp': jax.random.normal(ks[1], (B, S, DIM), jnp.float32), 'Wq': jax.random.normal(ks[2], (DIM, DIM), jnp.float32) * sc, 'bq': jnp.zeros((DIM,), jnp.float32), 'Wk': jax.random.normal(ks[3], (DIM, DIM), jnp.float32) * sc, 'bk': jnp.zeros((DIM,), jnp.float32), 'Wv': jax.random.normal(ks[4], (DIM, DIM), jnp.float32) * sc, 'bv': jnp.zeros((DIM,), jnp.float32), 'Wo': jax.random.normal(ks[5], (DIM, DIM), jnp.float32) * sc, 'bo': jnp.zeros((DIM,), jnp.float32), 'W1': jax.random.normal(ks[6], (DIM, FF), jnp.float32) * sc, 'b1': jnp.zeros((FF,), jnp.float32), 'W2': jax.random.normal(ks[7], (FF, DIM), jnp.float32) * (1.0 / np.sqrt(FF)), 'b2': jnp.zeros((DIM,), jnp.float32)}
        return inp
    _L1_xattn_all = _L1_xattn_setup()
    _L1_xattn_in = {k: v for k, v in _L1_xattn_all.items() if k in ('Wq', 'bq', 'Wk', 'bk', 'Wv', 'bv', 'Wo', 'bo', 'W1', 'b1', 'W2', 'b2')}
    del _L1_xattn_all

    def _L2_xattn_setup():
        import jax, jax.numpy as jnp
        import numpy as np
        NUM_ITERATIONS = 3
        LN_EPS = 1e-05
        key = jax.random.key(seed)
        ks = jax.random.split(key, 10)
        B, L, Lv, H = (8, 256, 32, 128)
        s = 1.0 / np.sqrt(H)
        s2 = 1.0 / np.sqrt(2 * H)
        return {'text_feat': jax.random.normal(ks[0], (B, L, H), dtype=jnp.float32), 'vision_feat': jax.random.normal(ks[1], (B, Lv, H), dtype=jnp.float32), 'Wt': jax.random.uniform(ks[2], (H, H), jnp.float32, -s, s), 'bt': jax.random.uniform(ks[3], (H,), jnp.float32, -s, s), 'Wv': jax.random.uniform(ks[4], (H, H), jnp.float32, -s, s), 'bv': jax.random.uniform(ks[5], (H,), jnp.float32, -s, s), 'Wg': jax.random.uniform(ks[6], (H, 2 * H), jnp.float32, -s2, s2), 'bg': jax.random.uniform(ks[7], (H,), jnp.float32, -s2, s2), 'gamma': jnp.ones((H,), jnp.float32), 'beta': jnp.zeros((H,), jnp.float32)}
    _L2_xattn_all = _L2_xattn_setup()
    _L2_xattn_in = {k: v for k, v in _L2_xattn_all.items() if k in ('Wt', 'bt', 'Wv', 'bv', 'Wg', 'bg', 'gamma', 'beta')}
    del _L2_xattn_all

    def _L3_xattn_setup():
        import jax, jax.numpy as jnp
        import numpy as np
        B, Q, KV = (2, 256, 256)
        D_MODEL = 128
        N_HEADS = 16
        D_KV = 64
        EPS = 1e-06
        key = jax.random.key(seed)
        ks = jax.random.split(key, 7)
        s = 0.02
        return {'hidden_states': jax.random.normal(ks[0], (B, Q, D_MODEL), jnp.float32), 'key_value_states': jax.random.normal(ks[1], (B, KV, D_MODEL), jnp.float32), 'wq': jax.random.normal(ks[2], (D_MODEL, N_HEADS * D_KV), jnp.float32) * s, 'wk': jax.random.normal(ks[3], (D_MODEL, N_HEADS * D_KV), jnp.float32) * s, 'wv': jax.random.normal(ks[4], (D_MODEL, N_HEADS * D_KV), jnp.float32) * s, 'wo': jax.random.normal(ks[5], (N_HEADS * D_KV, D_MODEL), jnp.float32) * s, 'norm_w': jnp.ones((D_MODEL,), jnp.float32)}
    _L3_xattn_all = _L3_xattn_setup()
    _L3_xattn_in = {k: v for k, v in _L3_xattn_all.items() if k in ('wq', 'wk', 'wv', 'wo', 'norm_w')}
    del _L3_xattn_all
    return {'x': x, 'ctx_1024': ctx_1024, 'L0_xattn_Wq': _L0_xattn_in['Wq'], 'L0_xattn_bq': _L0_xattn_in['bq'], 'L0_xattn_Wk': _L0_xattn_in['Wk'], 'L0_xattn_bk': _L0_xattn_in['bk'], 'L0_xattn_Wv': _L0_xattn_in['Wv'], 'L0_xattn_bv': _L0_xattn_in['bv'], 'L0_xattn_Wo': _L0_xattn_in['Wo'], 'L0_xattn_bo': _L0_xattn_in['bo'], 'L0_xattn_ln1_g': _L0_xattn_in['ln1_g'], 'L0_xattn_ln1_b': _L0_xattn_in['ln1_b'], 'L0_xattn_W1': _L0_xattn_in['W1'], 'L0_xattn_b1': _L0_xattn_in['b1'], 'L0_xattn_W2': _L0_xattn_in['W2'], 'L0_xattn_b2': _L0_xattn_in['b2'], 'L0_xattn_ln2_g': _L0_xattn_in['ln2_g'], 'L0_xattn_ln2_b': _L0_xattn_in['ln2_b'], 'L1_xattn_Wq': _L1_xattn_in['Wq'], 'L1_xattn_bq': _L1_xattn_in['bq'], 'L1_xattn_Wk': _L1_xattn_in['Wk'], 'L1_xattn_bk': _L1_xattn_in['bk'], 'L1_xattn_Wv': _L1_xattn_in['Wv'], 'L1_xattn_bv': _L1_xattn_in['bv'], 'L1_xattn_Wo': _L1_xattn_in['Wo'], 'L1_xattn_bo': _L1_xattn_in['bo'], 'L1_xattn_W1': _L1_xattn_in['W1'], 'L1_xattn_b1': _L1_xattn_in['b1'], 'L1_xattn_W2': _L1_xattn_in['W2'], 'L1_xattn_b2': _L1_xattn_in['b2'], 'L2_xattn_Wt': _L2_xattn_in['Wt'], 'L2_xattn_bt': _L2_xattn_in['bt'], 'L2_xattn_Wv': _L2_xattn_in['Wv'], 'L2_xattn_bv': _L2_xattn_in['bv'], 'L2_xattn_Wg': _L2_xattn_in['Wg'], 'L2_xattn_bg': _L2_xattn_in['bg'], 'L2_xattn_gamma': _L2_xattn_in['gamma'], 'L2_xattn_beta': _L2_xattn_in['beta'], 'L3_xattn_wq': _L3_xattn_in['wq'], 'L3_xattn_wk': _L3_xattn_in['wk'], 'L3_xattn_wv': _L3_xattn_in['wv'], 'L3_xattn_wo': _L3_xattn_in['wo'], 'L3_xattn_norm_w': _L3_xattn_in['norm_w']}

def reference(x, ctx_1024, L0_xattn_Wq, L0_xattn_bq, L0_xattn_Wk, L0_xattn_bk, L0_xattn_Wv, L0_xattn_bv, L0_xattn_Wo, L0_xattn_bo, L0_xattn_ln1_g, L0_xattn_ln1_b, L0_xattn_W1, L0_xattn_b1, L0_xattn_W2, L0_xattn_b2, L0_xattn_ln2_g, L0_xattn_ln2_b, L1_xattn_Wq, L1_xattn_bq, L1_xattn_Wk, L1_xattn_bk, L1_xattn_Wv, L1_xattn_bv, L1_xattn_Wo, L1_xattn_bo, L1_xattn_W1, L1_xattn_b1, L1_xattn_W2, L1_xattn_b2, L2_xattn_Wt, L2_xattn_bt, L2_xattn_Wv, L2_xattn_bv, L2_xattn_Wg, L2_xattn_bg, L2_xattn_gamma, L2_xattn_beta, L3_xattn_wq, L3_xattn_wk, L3_xattn_wv, L3_xattn_wo, L3_xattn_norm_w):
    import jax
    import jax.numpy as jnp

    def _L0_xattn_ref(query, key, values, Wq, bq, Wk, bk, Wv, bv, Wo, bo, ln1_g, ln1_b, W1, b1, W2, b2, ln2_g, ln2_b, mask):
        import jax, jax.numpy as jnp
        import numpy as np
        D_MODEL = 128
        N_HEADS = 16
        D_K = D_MODEL // N_HEADS
        D_FF = 512
        B, S = (2, 256)
        LN_EPS = 1e-05
        NEG_INF = -1e+30

        def layer_norm(x, g, b):
            mu = jnp.mean(x, axis=-1, keepdims=True)
            var = jnp.mean(jnp.square(x - mu), axis=-1, keepdims=True)
            return (x - mu) * jax.lax.rsqrt(var + LN_EPS) * g + b
        b, s, d = query.shape
        q = (query @ Wq + bq).reshape(b, s, N_HEADS, D_K).transpose(0, 2, 1, 3)
        k = (key @ Wk + bk).reshape(b, s, N_HEADS, D_K).transpose(0, 2, 1, 3)
        v = (values @ Wv + bv).reshape(b, s, N_HEADS, D_K).transpose(0, 2, 1, 3)
        scores = jnp.einsum('bhqd,bhkd->bhqk', q, k) / jnp.sqrt(jnp.float32(D_K))
        i = jnp.arange(s)[:, None]
        j = jnp.arange(s)[None, :]
        allowed = j < i + mask
        scores = jnp.where(allowed, scores, NEG_INF)
        attn = jax.nn.softmax(scores, axis=-1)
        if mask == 0:
            attn = attn.at[:, :, 0, :].set(0.0)
        ctx = jnp.einsum('bhqk,bhkd->bhqd', attn, v)
        ctx = ctx.transpose(0, 2, 1, 3).reshape(b, s, d)
        attn_out = ctx @ Wo + bo
        x = layer_norm(query + attn_out, ln1_g, ln1_b)
        ffn = jax.nn.relu(x @ W1 + b1) @ W2 + b2
        out = layer_norm(x + ffn, ln2_g, ln2_b)
        return out

    def _L1_xattn_ref(x, inp, Wq, bq, Wk, bk, Wv, bv, Wo, bo, W1, b1, W2, b2):
        import jax, jax.numpy as jnp
        import numpy as np
        DIM = 128
        NUM_HEADS = 16
        HEAD_DIM = DIM // NUM_HEADS
        FF = 4 * DIM
        B, T, S = (8, 64, 512)

        def _perceiver_layer(x, inp, Wq, bq, Wk, bk, Wv, bv, Wo, bo, W1, b1, W2, b2):
            b, t, _ = x.shape
            s = inp.shape[1]
            q = (x @ Wq + bq).reshape(b, t, NUM_HEADS, HEAD_DIM)
            k = (inp @ Wk + bk).reshape(b, s, NUM_HEADS, HEAD_DIM)
            v = (inp @ Wv + bv).reshape(b, s, NUM_HEADS, HEAD_DIM)
            attn = jnp.einsum('bthd,bshd->bhts', q, k)
            attn = jax.nn.softmax(attn / jnp.sqrt(jnp.float32(HEAD_DIM)), axis=-1)
            out = jnp.einsum('bhts,bshd->bthd', attn, v).reshape(b, t, DIM)
            attn_out = out @ Wo + bo
            x = x + attn_out
            h = jax.nn.gelu(x @ W1 + b1, approximate=True)
            x = x + (h @ W2 + b2)
            return x
        return _perceiver_layer(x, inp, Wq, bq, Wk, bk, Wv, bv, Wo, bo, W1, b1, W2, b2)

    def _L2_xattn_ref(text_feat, vision_feat, Wt, bt, Wv, bv, Wg, bg, gamma, beta):
        import jax, jax.numpy as jnp
        import numpy as np
        NUM_ITERATIONS = 3
        LN_EPS = 1e-05
        B, L, H = text_feat.shape
        vision_pooled = jnp.mean(vision_feat, axis=1, keepdims=True)
        text_proj = jnp.einsum('blh,oh->blo', text_feat, Wt) + bt
        vision_proj = jnp.einsum('bkh,oh->bko', vision_pooled, Wv) + bv
        vision_proj = jnp.broadcast_to(vision_proj, (B, L, H))
        agreement = jnp.sum(text_proj * vision_proj, axis=-1, keepdims=True)
        coupling = jnp.zeros((B, L, 1), dtype=text_feat.dtype)
        fused = text_feat
        for _ in range(NUM_ITERATIONS):
            routing_weights = jax.nn.softmax(coupling, axis=1)
            weighted_vision = routing_weights * vision_proj
            Wg_t, Wg_v = (Wg[:, :H], Wg[:, H:])
            gate_pre = jnp.einsum('blh,oh->blo', text_proj, Wg_t) + jnp.einsum('blh,oh->blo', weighted_vision, Wg_v) + bg
            gate = jax.nn.sigmoid(gate_pre)
            fused = text_feat + gate * weighted_vision
            coupling = coupling + agreement
        mu = jnp.mean(fused, axis=-1, keepdims=True)
        var = jnp.mean(jnp.square(fused - mu), axis=-1, keepdims=True)
        out = (fused - mu) / jnp.sqrt(var + LN_EPS) * gamma + beta
        return out

    def _L3_xattn_ref(hidden_states, key_value_states, wq, wk, wv, wo, norm_w):
        import jax, jax.numpy as jnp
        import numpy as np
        B, Q, KV = (2, 256, 256)
        D_MODEL = 128
        N_HEADS = 16
        D_KV = 64
        EPS = 1e-06
        var = jnp.mean(jnp.square(hidden_states), axis=-1, keepdims=True)
        normed = hidden_states * jax.lax.rsqrt(var + EPS) * norm_w
        b, q_len, _ = hidden_states.shape
        kv_len = key_value_states.shape[1]

        def split_heads(x):
            return x.reshape(b, -1, N_HEADS, D_KV).transpose(0, 2, 1, 3)
        q = split_heads(normed @ wq)
        k = split_heads(key_value_states @ wk)
        v = split_heads(key_value_states @ wv)
        scores = jnp.einsum('bhqd,bhkd->bhqk', q, k)
        attn = jax.nn.softmax(scores.astype(jnp.float32), axis=-1).astype(scores.dtype)
        ctx = jnp.einsum('bhqk,bhkd->bhqd', attn, v)
        ctx = ctx.transpose(0, 2, 1, 3).reshape(b, q_len, N_HEADS * D_KV)
        attn_out = ctx @ wo
        return hidden_states + attn_out
    x = _L0_xattn_ref(x, ctx_1024, ctx_1024, L0_xattn_Wq, L0_xattn_bq, L0_xattn_Wk, L0_xattn_bk, L0_xattn_Wv, L0_xattn_bv, L0_xattn_Wo, L0_xattn_bo, L0_xattn_ln1_g, L0_xattn_ln1_b, L0_xattn_W1, L0_xattn_b1, L0_xattn_W2, L0_xattn_b2, L0_xattn_ln2_g, L0_xattn_ln2_b, 0)
    x = _L1_xattn_ref(x, ctx_1024, L1_xattn_Wq, L1_xattn_bq, L1_xattn_Wk, L1_xattn_bk, L1_xattn_Wv, L1_xattn_bv, L1_xattn_Wo, L1_xattn_bo, L1_xattn_W1, L1_xattn_b1, L1_xattn_W2, L1_xattn_b2)
    x = _L2_xattn_ref(x, ctx_1024, L2_xattn_Wt, L2_xattn_bt, L2_xattn_Wv, L2_xattn_bv, L2_xattn_Wg, L2_xattn_bg, L2_xattn_gamma, L2_xattn_beta)
    x = _L3_xattn_ref(x, ctx_1024, L3_xattn_wq, L3_xattn_wk, L3_xattn_wv, L3_xattn_wo, L3_xattn_norm_w)
    return x

_drawn_inputs = setup_inputs


def setup_inputs(seed=0):
    import zlib

    import numpy as np

    out = dict(_drawn_inputs(seed))
    spreads = {'L0_xattn_bq': (0.0, 2.0),
     'L0_xattn_bk': (0.0, 2.0),
     'L0_xattn_bv': (0.0, 0.367),
     'L0_xattn_bo': (0.0, 0.1),
     'L0_xattn_ln1_g': (1.0, 0.2),
     'L0_xattn_ln1_b': (0.0, 0.1),
     'L0_xattn_b1': (0.0, 0.314),
     'L0_xattn_b2': (0.0, 0.1),
     'L0_xattn_ln2_g': (1.0, 0.2),
     'L0_xattn_ln2_b': (0.0, 0.1),
     'L1_xattn_bq': (0.0, 0.376),
     'L1_xattn_bk': (0.0, 2.0),
     'L1_xattn_bv': (0.0, 0.1),
     'L1_xattn_bo': (0.0, 0.1),
     'L1_xattn_b1': (0.0, 0.1),
     'L1_xattn_b2': (0.0, 0.1),
     'L2_xattn_gamma': (1.0, 0.2),
     'L2_xattn_beta': (0.0, 0.1),
     'L3_xattn_norm_w': (1.0, 0.6)}
    factors = {'L0_xattn_Wq': 8.0,
     'L0_xattn_Wk': 8.0,
     'L2_xattn_Wt': 5.759,
     'L2_xattn_bt': 50.008,
     'L2_xattn_Wv': 5.931,
     'L2_xattn_bv': 8.0,
     'L2_xattn_Wg': 8.0,
     'L2_xattn_bg': 200.0,
     'L3_xattn_wq': 4.677,
     'L3_xattn_wk': 4.718}
    for name, (base, spread) in spreads.items():
        noise = np.random.default_rng([zlib.crc32(name.encode()), seed]).standard_normal(out[name].shape)
        drawn = base * np.exp(spread * noise) if base else spread * noise
        out[name] = jnp.asarray(drawn.astype(out[name].dtype))
    for name, factor in factors.items():
        out[name] = (out[name] * factor).astype(out[name].dtype)
    return out
```

```python
from contextlib import ExitStack

import concourse.bass as bass
from concourse import mybir

F32 = mybir.dt.float32
BF16 = mybir.dt.bfloat16
ALU = mybir.AluOpType
ACT = mybir.ActivationFunctionType
AX = mybir.AxisListType

P = 128
B, L = 128, 64
GB = 8
TOK = GB * L
CH = TOK // P
G = B // GB
FT = 4
PAIRS = 8
LN_EPS = 1e-5
RMS_EPS = 1e-6
SCALE8 = 8.0 ** -0.5
NBANK = 8
NSLOT = 4
NSLOT_T = 2
DEPTH = 4

VEC = {n: i for i, n in enumerate(
    ["bq0", "bk0", "bv0", "bo0", "ln1_g", "ln1_b", "b2_0", "ln2_g", "ln2_b",
     "bq1", "bk1", "bv1", "bo1", "b2_1", "bt", "bvis", "bg", "norm_w"]
    + [f"b1_{l}_{j}" for l in range(2) for j in range(FT)])}
SQ = ["Wq0", "Wk0", "Wv0", "Wo0", "Wq1", "Wk1", "Wv1", "Wo1", "WtT", "WvisT", "WgtT", "WgvT"]
WCOL = {n: i * P for i, n in enumerate(SQ)}
_at = len(SQ) * P
for _n, _w in [("W1_0", 512), ("W2_0", 512), ("W1_1", 512), ("W2_1", 512),
               ("wq3", 1024), ("wk3", 1024), ("wv3", 1024), ("wo3", 1024)]:
    WCOL[_n] = _at
    _at += _w
WCOLS = _at
CCOL = {"ident": 0, "causal": 128, "m_sa": 192, "m_c": 196, "m_a": 200, "m_v": 202}
CCOLS = 202 + 128


def order(phase):
    chain = [("load",)]
    for l in range(2):
        chain += [("qk", l), ("v", l)] + [("pool",), ("vis",), ("gv",)] * (1 - l) +  [("att", l, s) for s in range(GB + DEPTH)] + [("attout", l)]
        if l == 0:
            chain += [("lnT", 0), ("lnZ", 0), ("lnF", 0)]
        chain += [("ffn", l)]
        if l == 0:
            chain += [("lnT", 1), ("lnZ", 1), ("lnF", 1)]
    chain += [("tp",), ("agree",), ("gate", 0), ("gate", 1), ("gate", 2),
              ("lnT", 2), ("lnZ", 2), ("lnY",), ("lnF", 2)]
    last = GB + DEPTH - 1
    finish = [("q3", p) for p in range(PAIRS)] + [("att3", s) for s in range(GB + DEPTH)] \
        + [("out3", k) for k in range(CH)]
    finish_after = {("load",): 3, ("qk", 0): 3, ("v", 0): 2,
                    ("att", 0, last - 2): 1, ("att", 0, last - 1): 1, ("att", 0, last): 1,
                    ("attout", 0): 1, ("lnT", 0): 2, ("lnZ", 0): 1, ("lnF", 0): 1, ("ffn", 0): 1,
                    ("lnT", 1): 2, ("lnZ", 1): 1, ("lnF", 1): 1, ("qk", 1): 1,
                    ("att", 1, last - 2): 1, ("att", 1, last - 1): 1}
    kv = [("k3", p) for p in range(PAIRS)] + [("v3", b) for b in range(GB)]
    kv_after = {("att", 1, last): 1, ("attout", 1): 1, ("ffn", 1): 1, ("tp",): 1, ("agree",): 2,
                ("gate", 0): 2, ("gate", 1): 2, ("gate", 2): 1, ("lnT", 2): 2, ("lnZ", 2): 2, ("lnY",): 1}
    if phase == "last":
        return finish
    weave(chain, kv, kv_after)
    if phase == "body":
        weave(chain, finish, finish_after)
    return chain


def weave(steps, fillers, after):
    assert sum(after.values()) == len(fillers)
    fillers = list(fillers)
    for step, n in after.items():
        i = steps.index(step) + 1
        steps[i:i] = fillers[:n]
        del fillers[:n]


def tiles_of(step):
    kind = step[0]
    if kind == "load":
        return ["xT", "cT"]
    if kind == "qk":
        return [("q", step[1]), ("k", step[1])]
    if kind == "v":
        return [("v", step[1], 0), ("v", step[1], 1)]
    if kind == "att":
        _, l, s = step
        return ([("S", l, s)] if s < GB else []) + ([("PT", l, s - 3)] if 0 <= s - 3 < GB else []) \
            + ([("O", l, (s - DEPTH) // 4)] if s >= DEPTH and (s - DEPTH) % 4 == 0 else [])
    if kind == "attout":
        return [("o", step[1])]
    if kind in ("lnT", "lnF"):
        return [step]
    if kind == "ffn":
        return [("h", step[1], j) for j in range(FT)] + [("f", step[1])]
    if kind == "vis":
        return ["vis"]
    if kind == "gv":
        return ["gv"]
    if kind == "tp":
        return ["tp"]
    if kind == "agree":
        return ["gp", "ag"]
    if kind in ("gate", "lnZ", "lnY", "pool"):
        return []
    if kind == "out3":
        return ["y3"] if step[1] == 0 else []
    if kind in ("k3", "v3", "q3"):
        return [step]
    if kind == "att3":
        s = step[1]
        return ([("PT3", s - 3)] if 0 <= s - 3 < GB else []) + ([("O3", s - DEPTH)] if s >= DEPTH else []) \
            + ([("S3", s)] if s < GB else [])
    raise KeyError(kind)


def read_by(tile):
    kind, rest = (tile, ()) if isinstance(tile, str) else (tile[0], tile[1:])
    if kind in ("S", "PT"):
        return {"S": "exp_ready", "PT": "probT_ready"}[kind], GB * rest[0] + rest[1] + 1
    if kind in ("q", "k"):
        return {"q": "qm_ready", "k": "km_ready"}[kind], rest[0] + 1
    if kind in ("v", "O"):
        return {"v": "vm_ready", "O": "ctx_half"}[kind], 2 * rest[0] + rest[1] + 1
    if kind in ("o", "f"):
        return "f_ready", 2 * rest[0] + (1 if kind == "o" else 2)
    if kind == "h":
        return "h_ready", FT * rest[0] + rest[1] + 1
    if kind == "lnT":
        return "z_ready", rest[0] + 1
    if kind == "lnF":
        return ("ln_out", rest[0] + 1) if rest[0] < 2 else ("ynT_ready", 1)
    if kind in ("k3", "v3", "q3", "S3", "PT3", "O3"):
        name = {"S3": "exp3_ready", "PT3": "prob3T_ready", "O3": "ctx3_ready"}.get(kind, kind + "_ready")
        return name, rest[0] + 1
    return {"xT": "xT_ready", "cT": "cT_ready", "vis": "vis_ready", "gv": "gv_ready", "tp": "tp_ready",
            "gp": "gate_b", "ag": "centred", "y3": "out_ready"}[kind], 1


FINISH_TILES = ("q3", "S3", "PT3", "O3", "y3")


BANKS = {"chain": (0, 1, 2, 3), "fill": (4, 5, 6), "values": (7,)}


def banks_for(tile):
    if tile[0] == "O":
        return "values"
    return "fill" if tile[0] in ("k3", "v3") or is_finish(tile) else "chain"


def is_finish(tile):
    return (tile if isinstance(tile, str) else tile[0]) in FINISH_TILES


class Signal:

    def __init__(self, sem, per_group):
        self.sem, self.per_group = sem, per_group

    def __call__(self, group, n):
        return self.sem, group * self.per_group + n


class Turn:

    ON_BANK, BANK = {}, {}
    TILES = {ph: [t for s in order(ph) for t in tiles_of(s)] for ph in ("first", "body", "last")}

    def __init__(self, phase, j=0):
        self.phase, self.j = phase, j
        self.chain = {"first": 0, "body": j + 1, "last": None}[phase]
        self.finish = {"first": None, "body": j, "last": G - 1}[phase]
        self.before = {"first": lambda b: 0,
                       "body": lambda b: self.uses("first", b) + j * self.uses("body", b),
                       "last": lambda b: self.uses("first", b) + (G - 1) * self.uses("body", b)}[phase]

    def bank_in(self, phase, tile):
        banks = BANKS[banks_for(tile)]
        tiles = [t for t in self.TILES[phase] if banks_for(t) == banks_for(tile)]
        return banks[(tiles.index(tile) - len(tiles)) % len(banks)]

    def on_bank(self, phase, b):
        if (phase, b) not in self.ON_BANK:
            self.ON_BANK[phase, b] = [t for t in self.TILES[phase] if self.bank_in(phase, t) == b]
        return self.ON_BANK[phase, b]

    def fillings(self, phase, b):
        return [t for t in self.on_bank(phase, b) if t[0] != "O"]

    def uses(self, phase, b):
        return len(self.fillings(phase, b))

    def bank(self, tile):
        if (self.phase, tile) not in self.BANK:
            self.BANK[self.phase, tile] = self.bank_in(self.phase, tile)
        return self.BANK[self.phase, tile]

    def filled(self, tile):
        b = self.bank(tile)
        return self.before(b) + self.fillings(self.phase, b).index(tile) + 1

    def previous(self, tile):
        b = self.bank(tile)
        tiles = self.on_bank(self.phase, b)
        i = tiles.index(tile)
        if i:
            old = tiles[i - 1]
            return old, self.finish if is_finish(old) else self.chain
        if self.phase == "first":
            return None, None
        old = self.on_bank("body", b)[-1]
        assert not is_finish(old) and old == self.on_bank("first", b)[-1]
        return old, self.finish


def xattn_sequence_kernel(nc, x, ctx_in, weights, vectors, gamma_rows, beta_rows, constants, out):
    with ExitStack() as stack:
        def sb(name, shape, dt=F32):
            return stack.enter_context(nc.sbuf_tensor(name, shape, dt))

        def sem(name):
            return stack.enter_context(nc.semaphore(name))

        wt = sb("wt", [P, WCOLS])
        vec = sb("vec", [P, len(VEC)])
        cst = sb("cst", [P, CCOLS])
        ident_b = sb("ident_b", [P, P], BF16)
        causal_b = sb("causal_b", [P, L], BF16)
        gamma = sb("gamma", [P, P])
        beta = sb("beta", [P, P])
        ones = sb("ones", [P, P])
        bqm = sb("bqm", [P, 2, 4])
        bg_half = sb("bg_half", [P, 1])
        half = sb("half", [P, CH])
        ln_eps = sb("ln_eps", [P, CH])
        rms_eps = sb("rms_eps", [P, CH])
        ident = cst[:, 0:P]

        def w(name, c0=0, n=P):
            return wt[:, WCOL[name] + c0:WCOL[name] + c0 + n]

        def v(name):
            return vec[:, VEC[name]:VEC[name] + 1]

        def c(name, k=0, n=1):
            return cst[:, CCOL[name] + k:CCOL[name] + k + n]

        x_in = sb("x_in", [P, CH, P])
        c_in = sb("c_in", [P, CH, P])
        y_out = sb("y_out", [P, CH, P])
        xT = sb("xT", [P, TOK])
        cT = sb("cT", [P, TOK])
        Qm = sb("Qm", [P, GB, 4, L])
        Km = sb("Km", [P, GB, 4, L])
        Vm = sb("Vm", [P, GB, P])
        half_ctx = sb("half_ctx", [P, 2, 4, L])
        aT = sb("aT", [P, GB, L])
        fT = sb("fT", [P, TOK])
        x1T = sb("x1T", [P, TOK])
        x2T = sb("x2T", [P, TOK])
        hT = sb("hT", [P, FT, TOK])
        stats = sb("stats", [P, CH, 6])
        stats_wait = sb("stats_wait", [P, 1])
        mv = sb("mv", [P, CH, 2])
        var_eps = sb("var_eps", [P, CH])
        rstd = sb("rstd", [P, CH])
        z = sb("z", [P, CH, P])
        pooled = sb("pooled", [P, GB])
        vis = sb("vis", [P, GB])
        gv = sb("gv", [P, GB])
        tpT = sb("tpT", [P, TOK])
        agree_in = sb("agree_in", [P, TOK])
        amax = sb("amax", [P, GB])
        asum = sb("asum", [P, GB])
        ainv = sb("ainv", [P, GB])
        route = sb("route", [P, TOK])
        gate = sb("gate", [P, TOK])
        y = sb("y", [P, CH, P])
        ynT = sb("ynT", [P, TOK])
        sq = sb("sq", [P, CH, P])
        msum = sb("msum", [P, CH])
        ms_eps = sb("ms_eps", [P, CH])
        rms = sb("rms", [P, CH])
        Q3 = sb("Q3", [P, PAIRS, GB, L])
        K3 = sb("K3", [P, PAIRS, GB, 2, L])
        V3 = sb("V3", [P, GB, PAIRS, 2, L])

        psum = [stack.enter_context(nc.psum_tensor(f"bank{i}", [P, 512], F32)) for i in range(NBANK)]
        bank_filled = [sem(f"bank_filled{i}") for i in range(NBANK)]

        signals = {}

        def signal(name, per_group):
            signals[name] = Signal(sem(name), per_group)
            return signals[name]

        x_loaded = signal("x_loaded", 32)
        y_out_free = signal("y_out_free", 16)
        out_ready = signal("out_ready", 1)
        xT_ready = signal("xT_ready", 1)
        cT_ready = signal("cT_ready", 1)
        qm_ready = signal("qm_ready", 2)
        km_ready = signal("km_ready", 2)
        vm_ready = signal("vm_ready", 4)
        pv_done = signal("pv_done", 16)
        half_ready = signal("half_ready", 4)
        ctx_half = signal("ctx_half", 4)
        aT_ready = signal("aT_ready", 1)
        f_ready = signal("f_ready", 5)
        h_ready = signal("h_ready", 2 * FT)
        stats_ready = signal("stats_ready", 3)
        mv_ready = signal("mv_ready", 3)
        var_ready = signal("var_ready", 3)
        rstd_ready = signal("rstd_ready", 3)
        z_ready = signal("z_ready", 3)
        ln_out = signal("ln_out", 2)
        x3_ready = signal("x3_ready", 1)
        pooled_ready = signal("pooled_ready", 1)
        vis_ready = signal("vis_ready", 1)
        gv_ready = signal("gv_ready", 1)
        tp_ready = signal("tp_ready", 1)
        agree_in_ready = signal("agree_in_ready", 1)
        amax_ready = signal("amax_ready", 1)
        centred = signal("centred", 1)
        agree_exp = signal("agree_exp", 1)
        asum_ready = signal("asum_ready", 1)
        ainv_ready = signal("ainv_ready", 1)
        route_ready = signal("route_ready", 1)
        gate_a = signal("gate_a", 1)
        gate_b = signal("gate_b", 1)
        gate_ready = signal("gate_ready", 1)
        gate_c = signal("gate_c", 1)
        gate_d = signal("gate_d", 1)
        y_a = signal("y_a", 1)
        y_ready = signal("y_ready", 1)
        square_done = signal("square_done", 1)
        ms_ready = signal("ms_ready", 1)
        rms_ready = signal("rms_ready", 1)
        yn_ready = signal("yn_ready", 1)
        ynT_ready = signal("ynT_ready", 1)
        k3_ready = signal("k3_ready", 8)
        v3_ready = signal("v3_ready", 8)
        q3_ready = signal("q3_ready", 8)
        ctx3_ready = signal("ctx3_ready", 8)

        class Softmax:

            def __init__(self, tag, per_group, scale):
                self.scale = scale
                self.prob = sb("prob" + tag, [P, NSLOT, 8, L])
                self.probT = sb("probT" + tag, [P, NSLOT_T, CH, P])
                self.negmax = sb("negmax" + tag, [P, NSLOT, 8], BF16)
                self.sums = sb("sums" + tag, [P, NSLOT, 8])
                self.rinv = sb("rinv" + tag, [P, NSLOT, 8])
                self.max_ready = signal(f"max{tag}_ready", per_group)
                self.shifted = signal(f"shifted{tag}", per_group)
                self.exp_ready = signal(f"exp{tag}_ready", per_group)
                self.sum_ready = signal(f"sum{tag}_ready", per_group)
                self.rinv_ready = signal(f"rinv{tag}_ready", per_group)
                self.norm_ready = signal(f"norm{tag}_ready", per_group)
                self.probT_ready = signal(f"prob{tag}T_ready", per_group)

        softmax01 = Softmax("", 2 * GB, SCALE8)
        softmax3 = Softmax("3", GB, 1.0)
        setup_loaded, setup_done = sem("setup_loaded"), sem("setup_done")

        def emptied(turn, tile):
            old, group = turn.previous(tile)
            if old is None:
                return None
            name, n = read_by(old)
            return signals[name](group, n)

        def filled(turn, tile):
            return bank_filled[turn.bank(tile)], turn.filled(tile)

        def run(eng, steps):
            for s in order("first"):
                steps(Turn("first"), s)
            with nc.Fori(0, G - 1, engines=(eng.engine,), hint_back_edge=True) as j:
                turn = Turn("body", j)
                for s in order("body"):
                    steps(turn, s)
            for s in order("last"):
                steps(Turn("last"), s)

        block = stack.enter_context(nc.Block())

        @block.sync
        def _(sp):
            sp.dma_start(wt[:, :], weights).then_inc(setup_loaded, 16)
            for dst, src in ((vec, vectors), (cst, constants), (gamma, gamma_rows)):
                sp.dma_start(dst[:, :], src).then_inc(setup_loaded, 16)
            sp.dma_start(beta[:, :], beta_rows).then_inc(y_out_free.sem, 16)

            def load(group):
                rows = x[bass.ds(group * TOK, TOK), :].rearrange("(c p) f -> p c f", p=P)
                sp.dma_start(x_in[:, :, :], rows).then_inc(x_loaded.sem, 16)
                rows = ctx_in[bass.ds(group * TOK, TOK), :].rearrange("(c p) f -> p c f", p=P)
                sp.dma_start(c_in[:, :, :], rows).then_inc(x_loaded.sem, 16)

            def store(group):
                sp.wait_ge(*out_ready(group, 1))
                rows = out[bass.ds(group * TOK, TOK), :].rearrange("(c p) f -> p c f", p=P)
                sp.dma_start(rows, y_out[:, :, :]).then_inc(y_out_free.sem, 16)

            load(0)
            sp.wait_ge(*xT_ready(0, 1))
            sp.wait_ge(*cT_ready(0, 1))
            load(1)
            with sp.Fori(0, G - 2) as j:
                store(j)
                sp.wait_ge(*xT_ready(j + 1, 1))
                sp.wait_ge(*cT_ready(j + 1, 1))
                load(j + 2)
            store(G - 2)
            store(G - 1)
            sp.wait_ge(y_out_free.sem, 16 * (G + 1))

        @block.tensor
        def _(pe):
            pe.wait_ge(setup_loaded, 16 * 4)
            pe.wait_ge(setup_done, 2)

            def fill(turn, tile, last):
                last.then_inc(bank_filled[turn.bank(tile)], 1)

            def mm(o, lhsT, rhs, start=True, stop=True):
                return nc.tensor.matmul(o, lhsT, rhs, start=start, stop=stop, skip_group_check=True)

            def linear(turn, tile, wname, src, c0=0):
                if emptied(turn, tile):
                    pe.wait_ge(*emptied(turn, tile))
                o = psum[turn.bank(tile)]
                fill(turn, tile, mm(o[:, :], w(wname, c0), src))

            def transpose4(turn, tile, src):
                if emptied(turn, tile):
                    pe.wait_ge(*emptied(turn, tile))
                o = psum[turn.bank(tile)]
                for k in range(CH):
                    last = nc.tensor.transpose(o[:, k * P:(k + 1) * P], src(k), ident)
                fill(turn, tile, last)

            def attention(turn, g, s, sm, n0, S_, PT_, scores, values):
                if s < GB and sm is not softmax3:
                    scores(s)
                if 0 <= s - 1 < GB:
                    b = s - 1
                    o = psum[turn.bank((*S_, b))]
                    pe.wait_ge(*sm.max_ready(g, n0 + b + 1))
                    mm(o[:, :], ident_b[:, :], sm.negmax[:, b % NSLOT, :].unsqueeze(2).broadcast_to([P, 8, L]),
                       start=False).then_inc(sm.shifted.sem, 1)
                if 0 <= s - 3 < GB:
                    b = s - 3
                    pe.wait_ge(*sm.norm_ready(g, n0 + b + 1))
                    pr = sm.prob[:, b % NSLOT].rearrange("p c k -> p (c k)")
                    transpose4(turn, (*PT_, b), lambda k: pr[:, k * P:(k + 1) * P])
                if s >= DEPTH:
                    b = s - DEPTH
                    pe.wait_ge(*sm.probT_ready(g, n0 + b + 1))
                    values(b)
                if s < GB and sm is softmax3:
                    scores(s)

            def steps(turn, step):
                kind, g = step[0], turn.chain
                if kind == "load":
                    pe.wait_ge(*x_loaded(g, 32))
                    transpose4(turn, "xT", lambda k: x_in[:, k, :])
                    transpose4(turn, "cT", lambda k: c_in[:, k, :])
                elif kind == "qk":
                    l = step[1]
                    if l == 0:
                        pe.wait_ge(*xT_ready(g, 1))
                        pe.wait_ge(*cT_ready(g, 1))
                    else:
                        pe.wait_ge(*ln_out(g, 2))
                    linear(turn, ("q", l), f"Wq{l}", xT[:, :] if l == 0 else x2T[:, :])
                    linear(turn, ("k", l), f"Wk{l}", cT[:, :])
                elif kind == "v":
                    l = step[1]
                    for hf in range(2):
                        if emptied(turn, ("v", l, hf)):
                            pe.wait_ge(*emptied(turn, ("v", l, hf)))
                        o = psum[turn.bank(("v", l, hf))]
                        for i in range(4):
                            b = 4 * hf + i
                            for c2 in range(2):
                                last = mm(o[64 * c2:64 * c2 + 64, i * P:(i + 1) * P],
                                          cT[:, b * L:(b + 1) * L], w(f"Wv{l}"))
                        fill(turn, ("v", l, hf), last)
                elif kind == "att":
                    l, s = step[1], step[2]

                    def scores(b):
                        if b == 0:
                            pe.wait_ge(*qm_ready(g, l + 1))
                            pe.wait_ge(*km_ready(g, l + 1))
                        tile = ("S", l, b)
                        if emptied(turn, tile):
                            pe.wait_ge(*emptied(turn, tile))
                        o = psum[turn.bank(tile)]
                        if l == 0:
                            mm(o[:, :], ident_b[:, :], causal_b[:, :].unsqueeze(1).broadcast_to([P, 8, L]),
                               stop=False)
                        for k in range(2):
                            last = mm(o[:, 256 * k:256 * (k + 1)],
                                      Qm[:, b, 2 * k:2 * k + 2, :].rearrange("p a q -> p (a q)"),
                                      Km[:, b, :, :].rearrange("p c k -> p (c k)"),
                                      start=(l == 1 and k == 0))
                        fill(turn, tile, last)

                    def values(b):
                        tile = ("O", l, b // 4)
                        if b == 0:
                            pe.wait_ge(*vm_ready(g, 2 * l + 2))
                        if b % 4 == 0 and emptied(turn, tile):
                            pe.wait_ge(*emptied(turn, tile))
                        o = psum[turn.bank(tile)]
                        for t in range(4):
                            last = mm(o[32 * t:32 * t + 32, (b % 4) * P:(b % 4 + 1) * P],
                                      Vm[:, b, 32 * t:32 * t + 32], softmax01.probT[:, b % NSLOT_T, t, :])
                        last.then_inc(pv_done.sem, 1)

                    attention(turn, g, s, softmax01, GB * l, ("S", l), ("PT", l), scores, values)
                elif kind == "attout":
                    l = step[1]
                    if l == 0:
                        pe.wait_ge(*aT_ready(g, 1))
                    else:
                        pe.wait_ge(*ctx_half(g, 4))
                    linear(turn, ("o", l), f"Wo{l}", aT[:, :, :].rearrange("p b q -> p (b q)"))
                elif kind == "lnT":
                    pe.wait_ge(*f_ready(g, {0: 1, 1: 2, 2: 5}[step[1]]))
                    transpose4(turn, step, lambda k: fT[:, k * P:(k + 1) * P])
                elif kind == "lnF":
                    if step[1] < 2:
                        pe.wait_ge(*z_ready(g, step[1] + 1))
                    else:
                        pe.wait_ge(*yn_ready(g, 1))
                    transpose4(turn, step, lambda k: z[:, k, :])
                elif kind == "ffn":
                    l = step[1]
                    if l == 0:
                        pe.wait_ge(*ln_out(g, 1))
                    else:
                        pe.wait_ge(*f_ready(g, 3))
                    for j in range(FT):
                        linear(turn, ("h", l, j), f"W1_{l}", (x1T if l == 0 else fT)[:, :], j * P)
                    if emptied(turn, ("f", l)):
                        pe.wait_ge(*emptied(turn, ("f", l)))
                    o = psum[turn.bank(("f", l))]
                    for j in range(FT):
                        pe.wait_ge(*h_ready(g, FT * l + j + 1))
                        last = mm(o[:, :], w(f"W2_{l}", j * P), hT[:, j, :], start=(j == 0), stop=(j == FT - 1))
                    fill(turn, ("f", l), last)
                elif kind == "vis":
                    pe.wait_ge(*pooled_ready(g, 1))
                    if emptied(turn, "vis"):
                        pe.wait_ge(*emptied(turn, "vis"))
                    o = psum[turn.bank("vis")]
                    fill(turn, "vis", mm(o[:, 0:GB], w("WvisT"), pooled[:, :]))
                elif kind == "gv":
                    pe.wait_ge(*vis_ready(g, 1))
                    if emptied(turn, "gv"):
                        pe.wait_ge(*emptied(turn, "gv"))
                    o = psum[turn.bank("gv")]
                    fill(turn, "gv", mm(o[:, 0:GB], w("WgvT"), vis[:, :]))
                elif kind == "tp":
                    pe.wait_ge(*f_ready(g, 4))
                    linear(turn, "tp", "WtT", x1T[:, :])
                elif kind == "agree":
                    pe.wait_ge(*tp_ready(g, 1))
                    linear(turn, "gp", "WgtT", tpT[:, :])
                    pe.wait_ge(*agree_in_ready(g, 1))
                    if emptied(turn, "ag"):
                        pe.wait_ge(*emptied(turn, "ag"))
                    o = psum[turn.bank("ag")]
                    fill(turn, "ag", mm(o[:, :], ones[:, :], agree_in[:, :]))
                elif kind == "k3":
                    linear(turn, step, "wk3", cT[:, :], step[1] * P)
                elif kind == "v3":
                    b = step[1]
                    if emptied(turn, step):
                        pe.wait_ge(*emptied(turn, step))
                    o = psum[turn.bank(step)]
                    for c2 in range(2):
                        wv = w("wv3", 0, 1024).rearrange("i (p g d) -> i g p d", g=2, d=L)[:, c2]
                        last = mm(o[64 * c2:64 * c2 + 64, :], cT[:, b * L:(b + 1) * L], wv)
                    fill(turn, step, last)
                elif kind == "q3":
                    pe.wait_ge(*ynT_ready(turn.finish, 1))
                    linear(turn, step, "wq3", ynT[:, :], step[1] * P)
                elif kind == "att3":
                    g3, s = turn.finish, step[1]

                    def scores3(b):
                        if b == 0:
                            pe.wait_ge(*q3_ready(g3, PAIRS))
                            pe.wait_ge(*k3_ready(g3, PAIRS))
                            pe.wait_ge(*v3_ready(g3, GB))
                        tile = ("S3", b)
                        if emptied(turn, tile):
                            pe.wait_ge(*emptied(turn, tile))
                        o = psum[turn.bank(tile)]
                        for t in range(4):
                            for a in range(2):
                                last = mm(o[64 * a:64 * a + 64, t * P:(t + 1) * P], Q3[:, 2 * t + a, b, :],
                                          K3[:, 2 * t + a, b, :, :].rearrange("p g k -> p (g k)"), start=(t == 0))
                        fill(turn, tile, last)

                    def values3(b):
                        tile = ("O3", b)
                        if emptied(turn, tile):
                            pe.wait_ge(*emptied(turn, tile))
                        o = psum[turn.bank(tile)]
                        for t in (3, 2, 1, 0):
                            mm(o[:, 64 * (3 + t):64 * (5 + t)], V3[:, b, 2 * t + 1].rearrange("p g d -> p (g d)"),
                               softmax3.probT[:, b % NSLOT_T, t, :])
                        for t in range(4):
                            n = P if t < 3 else L
                            last = mm(o[:, 64 * t:64 * t + n], V3[:, b, 2 * t].rearrange("p g d -> p (g d)"),
                                      softmax3.probT[:, b % NSLOT_T, t, 0:n])
                        fill(turn, tile, last)

                    attention(turn, g3, s, softmax3, 0, ("S3",), ("PT3",), scores3, values3)
                elif kind == "out3":
                    k = step[1]
                    if k == 0:
                        pe.wait_ge(*ctx3_ready(turn.finish, GB))
                        pe.wait_ge(*emptied(turn, "y3"))
                    o = psum[turn.bank("y3")]
                    for p in range(PAIRS):
                        last = mm(o[:, k * P:(k + 1) * P],
                                  Q3[:, p, 2 * k:2 * k + 2, :].rearrange("p b q -> p (b q)"),
                                  w("wo3", p * P), start=(p == 0), stop=(p == PAIRS - 1))
                    if k == CH - 1:
                        fill(turn, "y3", last)

            run(pe, steps)

        @block.scalar
        def _(act):
            act.wait_ge(setup_loaded, 16 * 4)
            act.wait_ge(setup_done, 2)

            def steps(turn, step):
                kind, g = step[0], turn.chain
                if kind == "load":
                    act.wait_ge(*filled(turn, "xT"))
                    o = psum[turn.bank("xT")]
                    nc.scalar.activation(xT[:, :], o[:, :], ACT.Identity).then_inc(xT_ready.sem, 1)
                elif kind == "qk":
                    l = step[1]
                    tile = ("q", l)
                    act.wait_ge(*filled(turn, tile))
                    o = psum[turn.bank(tile)]
                    for k in range(4):
                        last = nc.scalar.activation(Qm[:, :, k, :], o[:, :].rearrange("p (b q) -> p b q", b=GB),
                                                    ACT.Identity, bias=bqm[:, l, k:k + 1], scale=c("m_sa", k))
                    last.then_inc(qm_ready.sem, 1)
                elif kind in ("att", "att3"):
                    three = kind == "att3"
                    s = step[-1]
                    sm, grp, n0 = (softmax3, turn.finish, 0) if three else (softmax01, g, GB * step[1])
                    S_, PT_ = (("S3",), ("PT3",)) if three else (("S", step[1]), ("PT", step[1]))
                    if 0 <= s - 1 < GB:
                        b = s - 1
                        act.wait_ge(*sm.shifted(grp, n0 + b + 1))
                        o = psum[turn.bank((*S_, b))]
                        nc.scalar.activation(sm.prob[:, b % NSLOT].rearrange("p c k -> p (c k)"), o[:, :], ACT.Exp,
                                             scale=sm.scale).then_inc(sm.exp_ready.sem, 1)
                    if 0 <= s - 3 < GB:
                        b = s - 3
                        tile = (*PT_, b)
                        act.wait_ge(*filled(turn, tile))
                        if not three and n0 + b >= NSLOT_T:
                            act.wait_ge(*pv_done(grp, n0 + b + 1 - NSLOT_T))
                        o = psum[turn.bank(tile)]
                        nc.scalar.activation(sm.probT[:, b % NSLOT_T].rearrange("p t q -> p (t q)"), o[:, :],
                                             ACT.Identity).then_inc(sm.probT_ready.sem, 1)
                    if three and s >= DEPTH:
                        b = s - DEPTH
                        tile = ("O3", b)
                        act.wait_ge(*filled(turn, tile))
                        o = psum[turn.bank(tile)]
                        nc.scalar.activation(
                            Q3[:, :, b, :].rearrange("p (t a) q -> p a t q", a=2),
                            o[:, :].rearrange("p (a t q) -> p a t q", a=2, t=4), ACT.Identity
                        ).then_inc(ctx3_ready.sem, 1)
                elif kind == "lnF":
                    n = step[1]
                    act.wait_ge(*filled(turn, step))
                    o = psum[turn.bank(step)]
                    if n < 2:
                        dst = (x1T, x2T)[n]
                        nc.scalar.activation(dst[:, :], o[:, :], ACT.Identity, bias=v(f"ln{n + 1}_b"),
                                             scale=v(f"ln{n + 1}_g")).then_inc(ln_out.sem, 1)
                    else:
                        nc.scalar.activation(ynT[:, :], o[:, :], ACT.Identity,
                                             scale=v("norm_w")).then_inc(ynT_ready.sem, 1)
                elif kind == "lnZ" and step[1] == 2:
                    act.wait_ge(*y_ready(g, 1))
                    for k in range(CH):
                        last = nc.scalar.activation(sq[:, k, :], y[:, k, :], ACT.Square, scale=P ** -0.5,
                                                    accum_out=msum[:, k:k + 1])
                    last.then_inc(square_done.sem, 1)
                elif kind == "ffn":
                    l = step[1]
                    for j in range(FT):
                        tile = ("h", l, j)
                        act.wait_ge(*filled(turn, tile))
                        o = psum[turn.bank(tile)]
                        nc.scalar.activation(hT[:, j, :], o[:, :], ACT.Relu if l == 0 else ACT.Gelu_apprx_tanh,
                                             bias=v(f"b1_{l}_{j}")).then_inc(h_ready.sem, 1)
                elif kind == "tp":
                    act.wait_ge(*filled(turn, "tp"))
                    o = psum[turn.bank("tp")]
                    nc.scalar.activation(tpT[:, :], o[:, :], ACT.Identity, bias=v("bt")).then_inc(tp_ready.sem, 1)
                elif kind == "gate" and step[1] == 0:
                    act.wait_ge(*centred(g, 1))
                    nc.scalar.activation(route[:, :], agree_in[:, :], ACT.Exp, scale=2.0)\
                        .then_inc(agree_exp.sem, 1)
                elif kind == "gate" and step[1] == 1:
                    act.wait_ge(*gate_b(g, 1))
                    nc.scalar.activation(gate[:, :], tpT[:, :], ACT.Tanh, bias=bg_half[:, 0:1], scale=0.5)\
                        .then_inc(gate_ready.sem, 1)
                elif kind == "q3":
                    p = step[1]
                    act.wait_ge(*filled(turn, step))
                    o = psum[turn.bank(step)]
                    last = nc.scalar.activation(Q3[:, p].rearrange("p b q -> p (b q)"), o[:, :], ACT.Identity)
                    last.then_inc(q3_ready.sem, 1)
                elif kind == "k3":
                    p = step[1]
                    act.wait_ge(*filled(turn, step))
                    o = psum[turn.bank(step)]
                    for c2 in range(2):
                        h = slice(64 * c2, 64 * c2 + 64)
                        last = nc.scalar.activation(K3[h, p, :, c2, :], o[h, :].rearrange("d (b k) -> d b k", b=GB),
                                                    ACT.Identity)
                    last.then_inc(k3_ready.sem, 1)
                elif kind == "v3":
                    b = step[1]
                    act.wait_ge(*filled(turn, step))
                    o = psum[turn.bank(step)]
                    for c2 in range(2):
                        h = slice(64 * c2, 64 * c2 + 64)
                        last = nc.scalar.activation(V3[h, b, :, c2, :], o[h, :].rearrange("k (p d) -> k p d", p=PAIRS),
                                                    ACT.Identity)
                    last.then_inc(v3_ready.sem, 1)

            run(act, steps)

        @block.gpsimd
        def _(pool):
            pool.memset(V3[:, :, :, :, :], 0.0)
            pool.memset(half[:, :], -0.5)
            pool.memset(ln_eps[:, :], LN_EPS)
            pool.memset(rms_eps[:, :], RMS_EPS)
            pool.memset(ones[:, :], 1.0).then_inc(setup_done, 1)
            pool.wait_ge(setup_done, 2)

            def steps(turn, step):
                kind, g = step[0], turn.chain
                if kind in ("att", "att3"):
                    three = kind == "att3"
                    s = step[-1]
                    sm, grp, n0 = (softmax3, turn.finish, 0) if three else (softmax01, g, GB * step[1])
                    if 0 <= s - 2 < GB:
                        b = s - 2
                        pool.wait_ge(*sm.rinv_ready(grp, n0 + b + 1))
                        pr = sm.prob[:, b % NSLOT]
                        ri = sm.rinv[:, b % NSLOT, :].unsqueeze(2).broadcast_to([P, 8, L])
                        nc.gpsimd.tensor_tensor(pr, pr, ri, ALU.mult).then_inc(sm.norm_ready.sem, 1)
                elif kind == "lnT":
                    n = step[1]
                    pool.wait_ge(*mv_ready(g, n + 1))
                    nc.gpsimd.tensor_tensor(var_eps[:, :], mv[:, :, 1], ln_eps[:, :], ALU.add)\
                        .then_inc(var_ready.sem, 1)
                    pool.wait_ge(*var_ready(g, n + 1))
                    nc.gpsimd.tensor_tensor(rstd[:, :], var_eps[:, :], half[:, :], ALU.pow)\
                        .then_inc(rstd_ready.sem, 1)
                elif kind == "lnY":
                    pool.wait_ge(*square_done(g, 1))
                    nc.gpsimd.tensor_tensor(ms_eps[:, :], msum[:, :], rms_eps[:, :], ALU.add)\
                        .then_inc(ms_ready.sem, 1)
                    pool.wait_ge(*ms_ready(g, 1))
                    nc.gpsimd.tensor_tensor(rms[:, :], ms_eps[:, :], half[:, :], ALU.pow)\
                        .then_inc(rms_ready.sem, 1)

            run(pool, steps)

        @block.vector
        def _(dve):
            dve.memset(K3[:, :, :, :, :], 0.0)
            dve.wait_ge(setup_loaded, 16 * 4)
            dve.tensor_copy(ident_b[:, :], ident)
            dve.tensor_copy(causal_b[:, :], c("causal", 0, L))
            for l in range(2):
                dve.tensor_scalar(bqm[:, l, :], c("m_sa", 0, 4), v(f"bq{l}"), None, ALU.mult)
            dve.tensor_scalar(bg_half[:, :], v("bg"), 0.5, None, ALU.mult).then_inc(setup_done, 1)
            dve.wait_ge(setup_done, 2)

            def seqs(ap):
                return ap.rearrange("p (b q) -> p b q", b=GB)

            def over_tokens(ap):
                return ap[:, :].unsqueeze(2).broadcast_to([P, GB, L])

            def steps(turn, step):
                kind, g = step[0], turn.chain
                if kind == "load":
                    dve.wait_ge(*filled(turn, "cT"))
                    o = psum[turn.bank("cT")]
                    nc.vector.tensor_copy(cT[:, :], o[:, :]).then_inc(cT_ready.sem, 1)
                elif kind == "qk":
                    l = step[1]
                    dve.wait_ge(*filled(turn, ("k", l)))
                    o = psum[turn.bank(("k", l))]
                    for k in range(4):
                        last = nc.vector.tensor_scalar(Km[:, :, k, :], seqs(o[:, :]), v(f"bk{l}"), c("m_c", k),
                                                       ALU.add, ALU.mult)
                    last.then_inc(km_ready.sem, 1)
                elif kind == "v":
                    l = step[1]
                    for hf in range(2):
                        dve.wait_ge(*filled(turn, ("v", l, hf)))
                        o = psum[turn.bank(("v", l, hf))]
                        last = nc.vector.tensor_tensor(
                            Vm[:, 4 * hf:4 * hf + 4, :], o[:, :].rearrange("p (b f) -> p b f", b=4),
                            c("m_v", 0, P).unsqueeze(1).broadcast_to([P, 4, P]), ALU.mult)
                        last.then_inc(vm_ready.sem, 1)
                elif kind in ("att", "att3"):
                    three = kind == "att3"
                    s = step[-1]
                    sm, grp, n0 = (softmax3, turn.finish, 0) if three else (softmax01, g, GB * step[1])
                    if s < GB:
                        b = s
                        tile = ("S3", b) if three else ("S", step[1], b)
                        dve.wait_ge(*filled(turn, tile))
                        o = psum[turn.bank(tile)]
                        nc.vector.tensor_reduce(sm.negmax[:, b % NSLOT, :], o[:, :].rearrange("p (c k) -> p c k", c=8),
                                                AX.X, ALU.max, negate=True).then_inc(sm.max_ready.sem, 1)
                    if 0 <= s - 1 < GB:
                        b = s - 1
                        dve.wait_ge(*sm.exp_ready(grp, n0 + b + 1))
                        nc.vector.tensor_reduce(sm.sums[:, b % NSLOT, :], sm.prob[:, b % NSLOT], AX.X, ALU.add)\
                            .then_inc(sm.sum_ready.sem, 1)
                        dve.wait_ge(*sm.sum_ready(grp, n0 + b + 1))
                        if n0 + b >= NSLOT:
                            dve.wait_ge(*sm.norm_ready(grp, n0 + b + 1 - NSLOT))
                        nc.vector.reciprocal(sm.rinv[:, b % NSLOT, :], sm.sums[:, b % NSLOT, :])\
                            .then_inc(sm.rinv_ready.sem, 1)
                    if not three and s >= DEPTH and (s - DEPTH) % 4 == 3:
                        l, hf = step[1], (s - DEPTH) // 4
                        dve.wait_ge(*pv_done(g, n0 + 4 * hf + 4))
                        o = psum[turn.bank(("O", l, hf))][:, :].rearrange("p (b a q) -> p a b q", b=4, a=2)
                        nc.vector.tensor_scalar(half_ctx[:, hf], o[:, 0], c("m_a", 0), v(f"bv{l}"), ALU.mult, ALU.add)\
                            .then_inc(half_ready.sem, 1)
                        dve.wait_ge(*half_ready(g, 2 * l + hf + 1))
                        last = nc.vector.scalar_tensor_tensor(aT[:, 4 * hf:4 * hf + 4, :], o[:, 1], c("m_a", 1),
                                                              half_ctx[:, hf], ALU.mult, ALU.add)
                        last.then_inc(ctx_half.sem, 1)
                elif kind == "attout":
                    l = step[1]
                    if l == 0:
                        dve.wait_ge(*ctx_half(g, 2))
                        nc.vector.memset(aT[:, :, 0:1], 0.0).then_inc(aT_ready.sem, 1)
                    dve.wait_ge(*filled(turn, ("o", l)))
                    o = psum[turn.bank(("o", l))]
                    nc.vector.scalar_tensor_tensor(fT[:, :], o[:, :], v(f"bo{l}"), (xT if l == 0 else x2T)[:, :],
                                                   ALU.add, ALU.add).then_inc(f_ready.sem, 1)
                elif kind == "lnT":
                    n = step[1]
                    dve.wait_ge(*filled(turn, step))
                    o = psum[turn.bank(step)]
                    for k in range(CH):
                        last = nc.vector.bn_stats(stats[:, k, :], o[:, k * P:(k + 1) * P])
                    last.then_inc(stats_ready.sem, 1)
                    dve.wait_ge(*stats_ready(g, n + 1))
                    nc.vector.tensor_copy(stats_wait[:, :], stats[:, 0, 0:1])
                    for k in range(CH):
                        last = nc.vector.bn_aggr(mv[:, k, :], stats[:, k, :])
                    last.then_inc(mv_ready.sem, 1)
                elif kind == "lnZ":
                    n = step[1]
                    dve.wait_ge(*mv_ready(g, n + 1))
                    dve.wait_ge(*rstd_ready(g, n + 1))
                    o = psum[turn.bank(("lnT", n))]
                    for k in range(CH):
                        last = nc.vector.tensor_scalar(z[:, k, :], o[:, k * P:(k + 1) * P], mv[:, k, 0:1],
                                                       rstd[:, k:k + 1], ALU.subtract, ALU.mult)
                    last.then_inc(z_ready.sem, 1)
                    if n == 2:
                        dve.wait_ge(*z_ready(g, 3))
                        nc.vector.tensor_tensor(y[:, :, :], z[:, :, :],
                                                gamma[:, :].unsqueeze(1).broadcast_to([P, CH, P]), ALU.mult)\
                            .then_inc(y_a.sem, 1)
                        dve.wait_ge(*y_a(g, 1))
                        dve.wait_ge(y_out_free.sem, 16)
                        nc.vector.tensor_tensor(y[:, :, :], y[:, :, :],
                                                beta[:, :].unsqueeze(1).broadcast_to([P, CH, P]), ALU.add)\
                            .then_inc(y_ready.sem, 1)
                elif kind == "lnY":
                    dve.wait_ge(*y_ready(g, 1))
                    dve.wait_ge(*rms_ready(g, 1))
                    for k in range(CH):
                        last = nc.vector.tensor_scalar(z[:, k, :], y[:, k, :], rms[:, k:k + 1], None, ALU.mult)
                    last.then_inc(yn_ready.sem, 1)
                elif kind == "ffn":
                    l = step[1]
                    dve.wait_ge(*filled(turn, ("f", l)))
                    o = psum[turn.bank(("f", l))]
                    if l == 0:
                        nc.vector.scalar_tensor_tensor(fT[:, :], o[:, :], v("b2_0"), x1T[:, :], ALU.add, ALU.add)\
                            .then_inc(f_ready.sem, 1)
                    else:
                        nc.vector.scalar_tensor_tensor(x1T[:, :], o[:, :], v("b2_1"), fT[:, :], ALU.add, ALU.add)\
                            .then_inc(f_ready.sem, 1)
                elif kind == "pool":
                    dve.wait_ge(*cT_ready(g, 1))
                    nc.vector.tensor_reduce(pooled[:, :], seqs(cT[:, :]), AX.X, ALU.add)\
                        .then_inc(pooled_ready.sem, 1)
                elif kind == "vis":
                    dve.wait_ge(*filled(turn, "vis"))
                    o = psum[turn.bank("vis")]
                    nc.vector.tensor_scalar(vis[:, :], o[:, 0:GB], 1.0 / L, v("bvis"), ALU.mult, ALU.add)\
                        .then_inc(vis_ready.sem, 1)
                elif kind == "gv":
                    dve.wait_ge(*filled(turn, "gv"))
                    o = psum[turn.bank("gv")]
                    nc.vector.tensor_copy(gv[:, :], o[:, 0:GB]).then_inc(gv_ready.sem, 1)
                elif kind == "agree":
                    dve.wait_ge(*tp_ready(g, 1))
                    dve.wait_ge(*vis_ready(g, 1))
                    nc.vector.tensor_tensor(seqs(agree_in[:, :]), seqs(tpT[:, :]), over_tokens(vis), ALU.mult)\
                        .then_inc(agree_in_ready.sem, 1)
                elif kind == "gate" and step[1] == 0:
                    dve.wait_ge(*filled(turn, "ag"))
                    o = psum[turn.bank("ag")]
                    nc.vector.tensor_reduce(amax[:, :], seqs(o[:, :]), AX.X, ALU.max).then_inc(amax_ready.sem, 1)
                    dve.wait_ge(*amax_ready(g, 1))
                    nc.vector.tensor_tensor(seqs(agree_in[:, :]), seqs(o[:, :]), over_tokens(amax), ALU.subtract)\
                        .then_inc(centred.sem, 1)
                elif kind == "gate" and step[1] == 1:
                    dve.wait_ge(*agree_exp(g, 1))
                    nc.vector.tensor_reduce(asum[:, :], seqs(route[:, :]), AX.X, ALU.add).then_inc(asum_ready.sem, 1)
                    dve.wait_ge(*asum_ready(g, 1))
                    nc.vector.reciprocal(ainv[:, :], asum[:, :]).then_inc(ainv_ready.sem, 1)
                    dve.wait_ge(*ainv_ready(g, 1))
                    nc.vector.tensor_tensor(seqs(route[:, :]), seqs(route[:, :]), over_tokens(ainv), ALU.mult)\
                        .then_inc(route_ready.sem, 1)
                    dve.wait_ge(*route_ready(g, 1))
                    dve.wait_ge(*gv_ready(g, 1))
                    nc.vector.tensor_tensor(seqs(fT[:, :]), seqs(route[:, :]), over_tokens(gv), ALU.mult)\
                        .then_inc(gate_a.sem, 1)
                    dve.wait_ge(*gate_a(g, 1))
                    dve.wait_ge(*filled(turn, "gp"))
                    o = psum[turn.bank("gp")]
                    nc.vector.tensor_tensor(tpT[:, :], o[:, :], fT[:, :], ALU.add).then_inc(gate_b.sem, 1)
                elif kind == "gate" and step[1] == 2:
                    dve.wait_ge(*gate_ready(g, 1))
                    nc.vector.scalar_tensor_tensor(gate[:, :], gate[:, :], 1.0, route[:, :], ALU.add, ALU.mult)\
                        .then_inc(gate_c.sem, 1)
                    dve.wait_ge(*gate_c(g, 1))
                    nc.vector.tensor_tensor(seqs(gate[:, :]), seqs(gate[:, :]), over_tokens(vis), ALU.mult)\
                        .then_inc(gate_d.sem, 1)
                    dve.wait_ge(*gate_d(g, 1))
                    nc.vector.scalar_tensor_tensor(fT[:, :], gate[:, :], 0.5, x1T[:, :], ALU.mult, ALU.add)\
                        .then_inc(f_ready.sem, 1)
                elif kind == "out3" and step[1] == CH - 1:
                    dve.wait_ge(*filled(turn, "y3"))
                    o = psum[turn.bank("y3")]
                    dve.wait_ge(*y_out_free(turn.finish, 16))
                    nc.vector.tensor_tensor(y_out[:, :, :], o[:, :].rearrange("p (c f) -> p c f", c=CH),
                                            y[:, :, :], ALU.add).then_inc(out_ready.sem, 1)

            run(dve, steps)


def kernel(**inputs):
    import numpy as np
    import concourse.bacc as bacc
    from concourse.bass_utils import run_bass_kernel_spmd

    a = {k: np.asarray(val) for k, val in inputs.items()}
    l0, l1, l2, l3 = (lambda n: a["L0_xattn_" + n]), (lambda n: a["L1_xattn_" + n]), \
        (lambda n: a["L2_xattn_" + n]), (lambda n: a["L3_xattn_" + n])

    def rows_to_columns(m):
        n = m.shape[0] // P
        return m.reshape(n, P, m.shape[1]).transpose(1, 0, 2).reshape(P, -1)

    mats = {"Wq0": l0("Wq"), "Wk0": l0("Wk"), "Wv0": l0("Wv"), "Wo0": l0("Wo"),
            "Wq1": l1("Wq"), "Wk1": l1("Wk"), "Wv1": l1("Wv"), "Wo1": l1("Wo"),
            "WtT": l2("Wt").T, "WvisT": l2("Wv").T, "WgtT": l2("Wg")[:, :P].T, "WgvT": l2("Wg")[:, P:].T,
            "W1_0": l0("W1"), "W2_0": rows_to_columns(l0("W2")), "W1_1": l1("W1"), "W2_1": rows_to_columns(l1("W2")),
            "wq3": l3("wq"), "wk3": l3("wk"), "wv3": l3("wv"), "wo3": rows_to_columns(l3("wo"))}
    weights = np.ascontiguousarray(np.concatenate([mats[n] for n in WCOL], axis=1))
    vecs = {"bq0": l0("bq"), "bk0": l0("bk"), "bv0": l0("bv"), "bo0": l0("bo"), "ln1_g": l0("ln1_g"),
            "ln1_b": l0("ln1_b"), "b2_0": l0("b2"), "ln2_g": l0("ln2_g"), "ln2_b": l0("ln2_b"),
            "bq1": l1("bq"), "bk1": l1("bk"), "bv1": l1("bv"), "bo1": l1("bo"), "b2_1": l1("b2"),
            "bt": l2("bt"), "bvis": l2("bv"), "bg": l2("bg"), "norm_w": l3("norm_w")}
    for l, b1 in enumerate((l0("b1"), l1("b1"))):
        for j in range(FT):
            vecs[f"b1_{l}_{j}"] = b1[j * P:(j + 1) * P]
    vectors = np.ascontiguousarray(np.stack([vecs[n] for n in VEC], axis=1))

    f = np.arange(P)
    t, am, c2 = f // 32, (f // 16) % 2, (f // 8) % 2
    q, k = np.arange(P)[:, None] % L, np.arange(L)[None, :]
    constants = np.zeros((P, CCOLS), np.float32)
    constants[:, 0:P] = np.eye(P)
    constants[:, CCOL["causal"]:CCOL["causal"] + L] = np.where((k < q) | (q == 0), 0.0, -1e30)
    for i in range(4):
        constants[:, CCOL["m_sa"] + i] = (t // 2 == i // 2) & (am == i % 2)
        constants[:, CCOL["m_c"] + i] = (t % 2 == i // 2) & (c2 == i % 2)
    for i in range(2):
        constants[:, CCOL["m_a"] + i] = am == i
    constants[:, CCOL["m_v"]:CCOL["m_v"] + P] = c2[None, :] == (np.arange(P) // L)[:, None]

    arrays = {"x": np.ascontiguousarray(a["x"]).reshape(B * L, P),
              "ctx": np.ascontiguousarray(a["ctx_1024"]).reshape(B * L, P),
              "weights": weights, "vectors": vectors,
              "gamma": np.ascontiguousarray(np.broadcast_to(l2("gamma"), (P, P))),
              "beta": np.ascontiguousarray(np.broadcast_to(l2("beta"), (P, P))),
              "constants": constants}
    nc = bacc.Bacc("TRN2", target_bir_lowering=False, num_devices=1)
    args = [nc.dram_tensor("in_" + n, m.shape, mybir.dt.from_np(m.dtype), kind="ExternalInput").ap()
            for n, m in arrays.items()]
    args.append(nc.dram_tensor("out", (B * L, P), F32, kind="ExternalOutput").ap())
    xattn_sequence_kernel(nc, *args)
    r = run_bass_kernel_spmd(nc, [{"in_" + n: m for n, m in arrays.items()}], core_ids=[0])
    return r.results[0]["out"].reshape(B, L, P)
```

```python
from contextlib import ExitStack

import concourse.bass as bass
from concourse import mybir

F32 = mybir.dt.float32
F32R = mybir.dt.float32r
BF16 = mybir.dt.bfloat16
ALU = mybir.AluOpType
ACT = mybir.ActivationFunctionType
AX = mybir.AxisListType

P = 128
B, L = 128, 64
GB = 8
TOK = GB * L
CH = TOK // P
G = B // GB
FT = 4
PAIRS = 8
LN_EPS = 1e-5
RMS_EPS = 1e-6
SCALE8 = 8.0 ** -0.5
NBANK = 8
NSLOT = 4
NSLOT_T = 2
DEPTH = 4

VEC = {n: i for i, n in enumerate(
    ["bq0", "bk0", "bv0", "bo0", "ln1_g", "ln1_b", "b2_0", "ln2_g", "ln2_b",
     "bq1", "bk1", "bv1", "bo1", "b2_1", "bt", "bvis", "bg", "gamma", "beta", "norm_w"]
    + [f"b1_{l}_{j}" for l in range(2) for j in range(FT)])}
SQ = ["Wq0", "Wv0", "Wo0", "Wq1", "Wv1", "Wo1", "WtT", "WvisT", "WgtT", "WgvT"]
WCOL = {n: i * P for i, n in enumerate(SQ)}
_at = len(SQ) * P
for _n, _w in [("W1_0", 512), ("W2_0", 512), ("W1_1", 512), ("W2_1", 512), ("wo3", 1024)]:
    WCOL[_n] = _at
    _at += _w
WCOLS = _at
SPLIT = {"Wk0": 0, "Wk1": 128, "wk3": 256, "wv3": 1280, "wq3": 2304}
SPLIT_COLS = 3328
SQ_COLS, FIRST_SPLIT = len(SQ) * P, 2 * P
CCOL = {"ident": 0, "causal": 128, "m_sa": 192, "m_c": 196, "m_a": 200, "m_v": 202, "rows": 330}
CCOLS = 330 + 128


def order(phase):
    chain = [("load",)]
    for l in range(2):
        chain += [("q", l)] + [("k", 0), ("v", 0)] * (1 - l) + [("att", l, s) for s in range(GB + DEPTH)] \
            + [("attout", l)]
        if l == 0:
            chain += [("lnT", 0), ("lnZ", 0), ("lnF", 0)]
        chain += [("ffn", l)]
        if l == 0:
            chain += [("lnT", 1), ("lnZ", 1), ("lnF", 1)]
    chain += [("tp",), ("agree",), ("gate", 0), ("gate", 1), ("gate", 2), ("lnT", 2), ("lnZ", 2), ("lnF", 2)]
    early = {("pool",): ("att", 0, 4), ("vis",): ("att", 0, 8), ("gv",): ("att", 0, 11),
             ("v", 1): ("q", 1), ("k", 1): ("lnZ", 1)}
    for step, before in early.items():
        chain.insert(chain.index(before) + 1, step)
    finish = [("rms",)] + [("q3", p) for p in range(PAIRS)] + [("rms_rows",)] + [("att3", s) for s in range(GB + DEPTH)] \
        + [("out3", k) for k in range(CH)]
    finish_after = {("k", 0): 1, ("att", 0, 0): 1, ("att", 0, 1): 1, ("att", 0, 4): 1,
                    ("att", 0, 7): 6, ("vis",): 1, ("att", 0, 9): 1, ("att", 0, 10): 1, ("gv",): 1,
                    ("attout", 0): 1, ("lnT", 0): 1, ("lnZ", 0): 1, ("lnF", 0): 1, ("ffn", 0): 2,
                    ("lnT", 1): 1, ("lnZ", 1): 1, ("lnF", 1): 1, ("q", 1): 1, ("att", 1, 7): 1,
                    ("att", 1, 8): 1}
    kv = [("k3", p) for p in range(PAIRS)] + [("v3", b) for b in range(GB)]
    kv_after = {("att", 1, 11): 2, ("ffn", 1): 1, ("tp",): 1, ("agree",): 1, ("gate", 0): 3,
                ("gate", 1): 2, ("gate", 2): 2, ("lnT", 2): 1, ("lnZ", 2): 3}
    if phase == "last":
        return finish
    weave(chain, kv, kv_after)
    if phase == "body":
        weave(chain, finish, finish_after)
    return chain


def weave(steps, fillers, after):
    assert sum(after.values()) == len(fillers)
    fillers = list(fillers)
    for step, n in after.items():
        i = steps.index(step) + 1
        steps[i:i] = fillers[:n]
        del fillers[:n]


def tiles_of(step):
    kind = step[0]
    if kind == "load":
        return ["xT", "cT"]
    if kind in ("q", "k"):
        return [step]
    if kind == "v":
        return [("v", step[1], 0), ("v", step[1], 1)]
    if kind == "att":
        _, l, s = step
        return ([("S", l, s)] if s < GB else []) + ([("PT", l, s - 3)] if 0 <= s - 3 < GB else []) \
            + ([("O", l, (s - DEPTH) // 4)] if s >= DEPTH and (s - DEPTH) % 4 == 0 else [])
    if kind == "attout":
        return [("o", step[1])]
    if kind in ("lnT", "lnF"):
        return [step]
    if kind == "ffn":
        return [("h", step[1], j) for j in range(FT)] + [("f", step[1])]
    if kind == "vis":
        return ["vis"]
    if kind == "gv":
        return ["gv"]
    if kind == "tp":
        return ["tp"]
    if kind == "agree":
        return ["gp", "ag"]
    if kind in ("gate", "lnZ", "rms", "pool"):
        return []
    if kind == "rms_rows":
        return ["rms_rows"]
    if kind == "out3":
        return ["y3"] if step[1] == 0 else []
    if kind in ("k3", "v3", "q3"):
        return [step]
    if kind == "att3":
        s = step[1]
        return ([("PT3", s - 3)] if 0 <= s - 3 < GB else []) + ([("O3", s - DEPTH)] if s >= DEPTH else []) \
            + ([("S3", s)] if s < GB else [])
    raise KeyError(kind)


def read_by(tile):
    kind, rest = (tile, ()) if isinstance(tile, str) else (tile[0], tile[1:])
    if kind in ("S", "PT"):
        return {"S": "exp_ready", "PT": "probT_ready"}[kind], GB * rest[0] + rest[1] + 1
    if kind in ("q", "k"):
        return {"q": "qm_ready", "k": "km_ready"}[kind], rest[0] + 1
    if kind in ("v", "O"):
        return {"v": "vm_ready", "O": "ctx_half"}[kind], 2 * rest[0] + rest[1] + 1
    if kind in ("o", "f"):
        return "f_ready", 2 * rest[0] + (1 if kind == "o" else 2)
    if kind == "h":
        return "h_ready", FT * rest[0] + rest[1] + 1
    if kind == "lnT":
        return "ln_centred", rest[0] + 1
    if kind == "lnF":
        return ("ln_out", rest[0] + 1) if rest[0] < 2 else ("yn_ready", 1)
    if kind in ("k3", "v3", "q3", "S3", "PT3", "O3"):
        name = {"S3": "exp3_ready", "PT3": "prob3T_ready", "O3": "ctx3_ready"}.get(kind, kind + "_ready")
        return name, rest[0] + 1
    return {"xT": "xT_ready", "cT": "cT_ready", "vis": "vis_ready", "gv": "gv_ready", "tp": "tp_ready",
            "gp": "gate_b", "ag": "centred", "y3": "out_ready",
            "rms_rows": "rms_rows_ready"}[kind], 1


FINISH_TILES = ("q3", "rms_rows", "S3", "PT3", "O3", "y3")


BANKS = {"chain": (0, 1, 2, 3), "fill": (4, 5, 6), "values": (7,)}


def banks_for(tile):
    if tile[0] == "O":
        return "values"
    return "fill" if tile[0] in ("k3", "v3") or is_finish(tile) else "chain"


def is_finish(tile):
    return (tile if isinstance(tile, str) else tile[0]) in FINISH_TILES


class Signal:

    def __init__(self, sem, per_group):
        self.sem, self.per_group = sem, per_group

    def __call__(self, group, n):
        return self.sem, group * self.per_group + n


class Turn:

    ON_BANK, BANK = {}, {}
    TILES = {ph: [t for s in order(ph) for t in tiles_of(s)] for ph in ("first", "body", "last")}

    def __init__(self, phase, j=0):
        self.phase, self.j = phase, j
        self.chain = {"first": 0, "body": j + 1, "last": None}[phase]
        self.finish = {"first": None, "body": j, "last": G - 1}[phase]
        self.before = {"first": lambda b: 0,
                       "body": lambda b: self.uses("first", b) + j * self.uses("body", b),
                       "last": lambda b: self.uses("first", b) + (G - 1) * self.uses("body", b)}[phase]

    def bank_in(self, phase, tile):
        banks = BANKS[banks_for(tile)]
        tiles = [t for t in self.TILES[phase] if banks_for(t) == banks_for(tile)]
        return banks[(tiles.index(tile) - len(tiles)) % len(banks)]

    def on_bank(self, phase, b):
        if (phase, b) not in self.ON_BANK:
            self.ON_BANK[phase, b] = [t for t in self.TILES[phase] if self.bank_in(phase, t) == b]
        return self.ON_BANK[phase, b]

    def fillings(self, phase, b):
        return [t for t in self.on_bank(phase, b) if t[0] != "O"]

    def uses(self, phase, b):
        return len(self.fillings(phase, b))

    def bank(self, tile):
        if (self.phase, tile) not in self.BANK:
            self.BANK[self.phase, tile] = self.bank_in(self.phase, tile)
        return self.BANK[self.phase, tile]

    def filled(self, tile):
        b = self.bank(tile)
        return self.before(b) + self.fillings(self.phase, b).index(tile) + 1

    def previous(self, tile):
        b = self.bank(tile)
        tiles = self.on_bank(self.phase, b)
        i = tiles.index(tile)
        if i:
            old = tiles[i - 1]
            return old, self.finish if is_finish(old) else self.chain
        if self.phase == "first":
            return None, None
        old = self.on_bank("body", b)[-1]
        assert not is_finish(old) and old == self.on_bank("first", b)[-1]
        return old, self.finish


def xattn_sequence_kernel(nc, x, ctx_in, weights, split_weights, vectors, gamma_rows, beta_rows, constants, out):
    with ExitStack() as stack:
        def sb(name, shape, dt=F32):
            return stack.enter_context(nc.sbuf_tensor(name, shape, dt))

        def sem(name):
            return stack.enter_context(nc.semaphore(name))

        wt = sb("wt", [P, WCOLS])
        w_high = sb("w_high", [P, SPLIT_COLS], F32R)
        w_low = sb("w_low", [P, SPLIT_COLS], F32R)
        vec = sb("vec", [P, len(VEC)])
        cst = sb("cst", [P, CCOLS])
        ident_b = sb("ident_b", [P, P], BF16)
        causal_b = sb("causal_b", [P, L], BF16)
        gamma = sb("gamma", [P, P])
        beta = sb("beta", [P, P])
        ones = sb("ones", [P, P])
        bqm = sb("bqm", [P, 2, 4])
        bg_half = sb("bg_half", [P, 1])
        yn_scale = sb("yn_scale", [P, 2])
        half = sb("half", [P, CH])
        ln_eps = sb("ln_eps", [P, CH])
        rms_eps = sb("rms_eps", [P, CH])
        ident = cst[:, 0:P]

        def w(name, c0=0, n=P):
            return wt[:, WCOL[name] + c0:WCOL[name] + c0 + n]

        def w_split(name, c0=0, n=P):
            at = SPLIT[name] + c0
            return w_high[:, at:at + n], w_low[:, at:at + n]

        def v(name):
            return vec[:, VEC[name]:VEC[name] + 1]

        def c(name, k=0, n=1):
            return cst[:, CCOL[name] + k:CCOL[name] + k + n]

        x_in = sb("x_in", [P, CH, P])
        c_in = sb("c_in", [P, CH, P])
        xT = sb("xT", [P, TOK])
        cT = sb("cT", [P, TOK])
        c_high = sb("c_high", [P, TOK + L], F32R)
        c_low = sb("c_low", [P, TOK + L], F32R)
        Qm = sb("Qm", [P, GB, 4, L])
        Km = sb("Km", [P, GB, 4, L])
        Vm = sb("Vm", [P, GB, P])
        half_ctx = sb("half_ctx", [P, 2, 4, L])
        aT = sb("aT", [P, GB, L])
        fT = sb("fT", [P, TOK])
        x1T = sb("x1T", [P, TOK])
        x2T = sb("x2T", [P, TOK])
        hT = Km[:, :, :, :].rearrange("p b c k -> p (b c k)").rearrange("p (j n) -> p j n", j=FT)
        stats = sb("stats", [P, CH, 6])
        stats_wait = sb("stats_wait", [P, 1])
        mv = sb("mv", [P, CH, 2])
        var_eps = sb("var_eps", [P, CH])
        rstd = sb("rstd", [P, CH])
        table_scratch = sb("table_scratch", [P, 1])
        z = sb("z", [P, CH, P])
        pooled = sb("pooled", [P, GB])
        vis = sb("vis", [P, GB])
        gv = sb("gv", [P, GB])
        tpT, agree_in, route, gate = (
            Qm[:, :, :, :].rearrange("p b a q -> p (b a q)")[:, i * TOK:(i + 1) * TOK] for i in range(4))
        amax = sb("amax", [P, GB])
        asum = sb("asum", [P, GB])
        ainv = sb("ainv", [P, GB])
        gv_route = sb("gv_route", [P, GB])
        vis_route = sb("vis_route", [P, GB])
        y = sb("y", [P, CH, P])
        yn_high = sb("yn_high", [P, TOK], F32R)
        yn_low = sb("yn_low", [P, TOK], F32R)
        msum = sb("msum", [P, CH])
        ms_eps = sb("ms_eps", [P, CH])
        rms = sb("rms", [P, CH])
        rms_own = sb("rms_own", [P, CH, 2])
        rms_rows = sb("rms_rows", [P, GB])
        Q3 = sb("Q3", [P, PAIRS, GB, L])
        K3 = sb("K3", [P, PAIRS, GB, 2, L])
        V3 = sb("V3", [P, GB, PAIRS, 2, L])
        w_stage = Q3[:, :, :, :].rearrange("p a b q -> p (a b q)")[:, 0:SPLIT_COLS]

        psum = [stack.enter_context(nc.psum_tensor(f"bank{i}", [P, 512], F32)) for i in range(NBANK)]
        bank_filled = [sem(f"bank_filled{i}") for i in range(NBANK)]

        signals = {}

        def signal(name, per_group):
            signals[name] = Signal(sem(name), per_group)
            return signals[name]

        x_loaded = signal("x_loaded", 32)
        y_free = signal("y_free", 16)
        out_ready = signal("out_ready", 1)
        xT_ready = signal("xT_ready", 1)
        cT_ready = signal("cT_ready", 1)
        c_high_ready = signal("c_high_ready", 1)
        c_low_ready = signal("c_low_ready", 1)
        qm_ready = signal("qm_ready", 2)
        km_ready = signal("km_ready", 2)
        vm_ready = signal("vm_ready", 4)
        pv_done = signal("pv_done", 16)
        half_ready = signal("half_ready", 4)
        ctx_half = signal("ctx_half", 4)
        f_ready = signal("f_ready", 5)
        h_ready = signal("h_ready", 2 * FT)
        stats_ready = signal("stats_ready", 3)
        mv_ready = signal("mv_ready", 3)
        var_ready = signal("var_ready", 3)
        rstd_ready = signal("rstd_ready", 3)
        ln_centred = signal("ln_centred", 3)
        z_ready = signal("z_ready", 3)
        ln_out = signal("ln_out", 2)
        x3_ready = signal("x3_ready", 1)
        pooled_ready = signal("pooled_ready", 1)
        vis_ready = signal("vis_ready", 1)
        gv_ready = signal("gv_ready", 1)
        tp_ready = signal("tp_ready", 1)
        agree_in_ready = signal("agree_in_ready", 1)
        amax_ready = signal("amax_ready", 1)
        centred = signal("centred", 1)
        agree_exp = signal("agree_exp", 1)
        asum_ready = signal("asum_ready", 1)
        ainv_ready = signal("ainv_ready", 1)
        route_ready = signal("route_ready", 1)
        gate_a = signal("gate_a", 1)
        gate_b = signal("gate_b", 1)
        gate_ready = signal("gate_ready", 1)
        gate_c = signal("gate_c", 1)
        gv_route_ready = signal("gv_route_ready", 1)
        vis_route_ready = signal("vis_route_ready", 1)
        y_a = signal("y_a", 1)
        y_ready = signal("y_ready", 1)
        square_done = signal("square_done", 1)
        ms_ready = signal("ms_ready", 1)
        rms_ready = signal("rms_ready", 1)
        yn_ready = signal("yn_ready", 1)
        yn_high_ready = signal("yn_high_ready", 1)
        rms_own_ready = signal("rms_own_ready", 1)
        rms_rows_ready = signal("rms_rows_ready", 1)
        yn_low_ready = signal("yn_low_ready", 1)
        k3_ready = signal("k3_ready", 8)
        v3_ready = signal("v3_ready", 8)
        q3_ready = signal("q3_ready", 8)
        ctx3_ready = signal("ctx3_ready", 8)

        class Softmax:

            def __init__(self, tag, per_group):
                self.prob = sb("prob" + tag, [P, NSLOT, 8, L])
                self.probT = sb("probT" + tag, [P, NSLOT_T, CH, P])
                self.negmax = sb("negmax" + tag, [P, NSLOT, 8], BF16)
                self.sums = sb("sums" + tag, [P, NSLOT, 8])
                self.rinv = sb("rinv" + tag, [P, NSLOT, 8])
                self.max_ready = signal(f"max{tag}_ready", per_group)
                self.shifted = signal(f"shifted{tag}", per_group)
                self.exp_ready = signal(f"exp{tag}_ready", per_group)
                self.sum_ready = signal(f"sum{tag}_ready", per_group)
                self.rinv_ready = signal(f"rinv{tag}_ready", per_group)
                self.norm_ready = signal(f"norm{tag}_ready", per_group)
                self.probT_ready = signal(f"prob{tag}T_ready", per_group)

        softmax01 = Softmax("", 2 * GB)
        softmax3 = Softmax("3", GB)
        constants_loaded, squares_loaded, rest_loaded = (
            sem("constants_loaded"), sem("squares_loaded"), sem("rest_loaded"))
        split_first_loaded, split_rest_loaded = sem("split_first_loaded"), sem("split_rest_loaded")
        high_first, low_first, high_rest, low_rest = (
            sem("high_first"), sem("low_first"), sem("high_rest"), sem("low_rest"))
        constants_done, keys_cleared, values_cleared = (
            sem("constants_done"), sem("keys_cleared"), sem("values_cleared"))

        def emptied(turn, tile):
            old, group = turn.previous(tile)
            if old is None:
                return None
            name, n = read_by(old)
            return signals[name](group, n)

        def filled(turn, tile):
            return bank_filled[turn.bank(tile)], turn.filled(tile)

        def run(eng, steps):
            for s in order("first"):
                steps(Turn("first"), s)
            with nc.Fori(0, G - 1, engines=(eng.engine,), hint_back_edge=True) as j:
                turn = Turn("body", j)
                for s in order("body"):
                    steps(turn, s)
            for s in order("last"):
                steps(Turn("last"), s)

        block = stack.enter_context(nc.Block())

        @block.sync
        def _(sp):
            def load(group):
                rows = x[bass.ds(group * TOK, TOK), :].rearrange("(c p) f -> p c f", p=P)
                sp.dma_start(x_in[:, :, :], rows).then_inc(x_loaded.sem, 16)
                rows = ctx_in[bass.ds(group * TOK, TOK), :].rearrange("(c p) f -> p c f", p=P)
                sp.dma_start(c_in[:, :, :], rows).then_inc(x_loaded.sem, 16)

            def store(group):
                sp.wait_ge(*out_ready(group, 1))
                rows = out[bass.ds(group * TOK, TOK), :].rearrange("(c p) f -> p c f", p=P)
                sp.dma_start(rows, y[:, :, :]).then_inc(y_free.sem, 16)

            sp.dma_start(cst[:, :], constants).then_inc(constants_loaded, 16)
            load(0)
            sp.dma_start(vec[:, :], vectors).then_inc(constants_loaded, 16)
            sp.dma_start(wt[:, 0:SQ_COLS], weights[:, 0:SQ_COLS]).then_inc(squares_loaded, 16)
            sp.dma_start(w_stage[:, 0:FIRST_SPLIT], split_weights[:, 0:FIRST_SPLIT]).then_inc(split_first_loaded, 16)
            sp.dma_start(w_stage[:, FIRST_SPLIT:], split_weights[:, FIRST_SPLIT:]).then_inc(split_rest_loaded, 16)
            sp.dma_start(wt[:, SQ_COLS:], weights[:, SQ_COLS:]).then_inc(rest_loaded, 16)
            sp.dma_start(gamma[:, :], gamma_rows).then_inc(rest_loaded, 16)
            sp.dma_start(beta[:, :], beta_rows).then_inc(y_free.sem, 16)
            sp.wait_ge(*xT_ready(0, 1))
            sp.wait_ge(*c_low_ready(0, 1))
            load(1)
            with sp.Fori(0, G - 2) as j:
                store(j)
                sp.wait_ge(*xT_ready(j + 1, 1))
                sp.wait_ge(*c_low_ready(j + 1, 1))
                load(j + 2)
            store(G - 2)
            store(G - 1)
            sp.wait_ge(y_free.sem, 16 * (G + 1))

        @block.tensor
        def _(pe):
            pe.wait_ge(constants_loaded, 16 * 2)

            def fill(turn, tile, last):
                last.then_inc(bank_filled[turn.bank(tile)], 1)

            def mm(o, lhsT, rhs, start=True, stop=True):
                return nc.tensor.matmul(o, lhsT, rhs, start=start, stop=stop, skip_group_check=True)

            def linear(turn, tile, wname, src, c0=0):
                if emptied(turn, tile):
                    pe.wait_ge(*emptied(turn, tile))
                o = psum[turn.bank(tile)]
                fill(turn, tile, mm(o[:, :], w(wname, c0), src))

            def split_mm(o, lhsT, rhs):
                mm(o, lhsT[0], rhs[0], stop=False)
                mm(o, lhsT[0], rhs[1], start=False, stop=False)
                return mm(o, lhsT[1], rhs[0], start=False)

            def split_linear(turn, tile, wname, src, c0=0):
                if emptied(turn, tile):
                    pe.wait_ge(*emptied(turn, tile))
                o = psum[turn.bank(tile)]
                fill(turn, tile, split_mm(o[:, :], w_split(wname, c0), src))

            def transpose4(turn, tile, src):
                if emptied(turn, tile):
                    pe.wait_ge(*emptied(turn, tile))
                o = psum[turn.bank(tile)]
                for k in range(CH):
                    last = nc.tensor.transpose(o[:, k * P:(k + 1) * P], src(k), ident)
                fill(turn, tile, last)

            def attention(turn, g, s, sm, n0, S_, PT_, scores, values):
                def shift(b):
                    o = psum[turn.bank((*S_, b))]
                    pe.wait_ge(*sm.max_ready(g, n0 + b + 1))
                    mm(o[:, :], ident_b[:, :], sm.negmax[:, b % NSLOT, :].unsqueeze(2).broadcast_to([P, 8, L]),
                       start=False).then_inc(sm.shifted.sem, 1)

                if s < GB and sm is softmax01:
                    scores(s)
                if 0 <= s - 1 < GB and sm is softmax01:
                    shift(s - 1)
                if 0 <= s - 3 < GB:
                    b = s - 3
                    pe.wait_ge(*sm.norm_ready(g, n0 + b + 1))
                    pr = sm.prob[:, b % NSLOT].rearrange("p c k -> p (c k)")
                    transpose4(turn, (*PT_, b), lambda k: pr[:, k * P:(k + 1) * P])
                if 0 <= s - 1 < GB and sm is softmax3:
                    shift(s - 1)
                if s >= DEPTH:
                    b = s - DEPTH
                    pe.wait_ge(*sm.probT_ready(g, n0 + b + 1))
                    values(b)
                if s < GB and sm is softmax3:
                    scores(s)

            def steps(turn, step):
                kind, g = step[0], turn.chain
                if kind == "load":
                    pe.wait_ge(*x_loaded(g, 32))
                    transpose4(turn, "xT", lambda k: x_in[:, k, :])
                    transpose4(turn, "cT", lambda k: c_in[:, k, :])
                elif kind == "q":
                    l = step[1]
                    if l == 0:
                        if turn.phase == "first":
                            pe.wait_ge(squares_loaded, 16)
                        pe.wait_ge(*xT_ready(g, 1))
                    else:
                        pe.wait_ge(*ln_out(g, 2))
                    linear(turn, ("q", l), f"Wq{l}", xT[:, :] if l == 0 else x2T[:, :])
                elif kind == "k":
                    l = step[1]
                    if l == 0:
                        pe.wait_ge(*c_low_ready(g, 1))
                        if turn.phase == "first":
                            pe.wait_ge(low_first, 1)
                    split_linear(turn, ("k", l), f"Wk{l}", (c_high[:, 0:TOK], c_low[:, 0:TOK]))
                elif kind == "v":
                    l = step[1]
                    if l == 0:
                        pe.wait_ge(*cT_ready(g, 1))
                    for hf in range(2):
                        if emptied(turn, ("v", l, hf)):
                            pe.wait_ge(*emptied(turn, ("v", l, hf)))
                        o = psum[turn.bank(("v", l, hf))]
                        for i in range(4):
                            b = 4 * hf + i
                            for c2 in range(2):
                                last = mm(o[64 * c2:64 * c2 + 64, i * P:(i + 1) * P],
                                          cT[:, b * L:(b + 1) * L], w(f"Wv{l}"))
                        fill(turn, ("v", l, hf), last)
                elif kind == "att":
                    l, s = step[1], step[2]

                    def scores(b):
                        if b == 0 and l == 0 and turn.phase == "first":
                            pe.wait_ge(constants_done, 2)
                        if b == 0:
                            pe.wait_ge(*qm_ready(g, l + 1))
                            pe.wait_ge(*km_ready(g, l + 1))
                        tile = ("S", l, b)
                        if emptied(turn, tile):
                            pe.wait_ge(*emptied(turn, tile))
                        o = psum[turn.bank(tile)]
                        if l == 0:
                            mm(o[:, :], ident_b[:, :], causal_b[:, :].unsqueeze(1).broadcast_to([P, 8, L]),
                               stop=False)
                        for k in range(2):
                            last = mm(o[:, 256 * k:256 * (k + 1)],
                                      Qm[:, b, 2 * k:2 * k + 2, :].rearrange("p a q -> p (a q)"),
                                      Km[:, b, :, :].rearrange("p c k -> p (c k)"),
                                      start=(l == 1 and k == 0))
                        fill(turn, tile, last)

                    def values(b):
                        tile = ("O", l, b // 4)
                        if b == 0:
                            pe.wait_ge(*vm_ready(g, 2 * l + 2))
                        if b % 4 == 0 and emptied(turn, tile):
                            pe.wait_ge(*emptied(turn, tile))
                        o = psum[turn.bank(tile)]
                        for t in range(4):
                            last = mm(o[32 * t:32 * t + 32, (b % 4) * P:(b % 4 + 1) * P],
                                      Vm[:, b, 32 * t:32 * t + 32], softmax01.probT[:, b % NSLOT_T, t, :])
                        last.then_inc(pv_done.sem, 1)

                    attention(turn, g, s, softmax01, GB * l, ("S", l), ("PT", l), scores, values)
                elif kind == "attout":
                    l = step[1]
                    pe.wait_ge(*ctx_half(g, 2 * l + 2))
                    linear(turn, ("o", l), f"Wo{l}", aT[:, :, :].rearrange("p b q -> p (b q)"))
                elif kind == "lnT":
                    pe.wait_ge(*f_ready(g, {0: 1, 1: 2, 2: 5}[step[1]]))
                    transpose4(turn, step, lambda k: fT[:, k * P:(k + 1) * P])
                elif kind == "lnF":
                    pe.wait_ge(*z_ready(g, step[1] + 1))
                    transpose4(turn, step, lambda k: z[:, k, :])
                elif kind == "ffn":
                    l = step[1]
                    if l == 0:
                        if turn.phase == "first":
                            pe.wait_ge(rest_loaded, 16 * 2)
                        pe.wait_ge(*ln_out(g, 1))
                    else:
                        pe.wait_ge(*f_ready(g, 3))
                    for j in range(FT):
                        linear(turn, ("h", l, j), f"W1_{l}", (x1T if l == 0 else fT)[:, :], j * P)
                    if emptied(turn, ("f", l)):
                        pe.wait_ge(*emptied(turn, ("f", l)))
                    o = psum[turn.bank(("f", l))]
                    for j in range(FT):
                        pe.wait_ge(*h_ready(g, FT * l + j + 1))
                        last = mm(o[:, :], w(f"W2_{l}", j * P), hT[:, j, :], start=(j == 0), stop=(j == FT - 1))
                    fill(turn, ("f", l), last)
                elif kind == "vis":
                    pe.wait_ge(*pooled_ready(g, 1))
                    if emptied(turn, "vis"):
                        pe.wait_ge(*emptied(turn, "vis"))
                    o = psum[turn.bank("vis")]
                    fill(turn, "vis", mm(o[:, 0:GB], w("WvisT"), pooled[:, :]))
                elif kind == "gv":
                    pe.wait_ge(*vis_ready(g, 1))
                    if emptied(turn, "gv"):
                        pe.wait_ge(*emptied(turn, "gv"))
                    o = psum[turn.bank("gv")]
                    fill(turn, "gv", mm(o[:, 0:GB], w("WgvT"), vis[:, :]))
                elif kind == "tp":
                    pe.wait_ge(*f_ready(g, 4))
                    linear(turn, "tp", "WtT", x1T[:, :])
                elif kind == "agree":
                    pe.wait_ge(*tp_ready(g, 1))
                    linear(turn, "gp", "WgtT", tpT[:, :])
                    pe.wait_ge(*agree_in_ready(g, 1))
                    if emptied(turn, "ag"):
                        pe.wait_ge(*emptied(turn, "ag"))
                    o = psum[turn.bank("ag")]
                    fill(turn, "ag", mm(o[:, :], ones[:, :], agree_in[:, :]))
                elif kind == "k3":
                    if turn.phase == "first" and step[1] == 0:
                        pe.wait_ge(low_rest, 1)
                    split_linear(turn, step, "wk3", (c_high[:, 0:TOK], c_low[:, 0:TOK]), step[1] * P)
                elif kind == "v3":
                    b = step[1]
                    two = slice(b * L, b * L + P)
                    if emptied(turn, step):
                        pe.wait_ge(*emptied(turn, step))
                    o = psum[turn.bank(step)]
                    fill(turn, step, split_mm(o[:, :], (c_high[:, two], c_low[:, two]),
                                              w_split("wv3", b % 2 * TOK, TOK)))
                elif kind == "q3":
                    pe.wait_ge(*yn_low_ready(turn.finish, 1))
                    split_linear(turn, step, "wq3", (yn_high[:, :], yn_low[:, :]), step[1] * P)
                elif kind == "rms_rows":
                    pe.wait_ge(*rms_own_ready(turn.finish, 1))
                    pe.wait_ge(*emptied(turn, "rms_rows"))
                    o = psum[turn.bank("rms_rows")]
                    fill(turn, "rms_rows", mm(o[:, 0:GB], c("rows", 0, P),
                                              rms_own[:, :, :].rearrange("p k e -> p (k e)")))
                elif kind == "att3":
                    g3, s = turn.finish, step[1]

                    def scores3(b):
                        if b == 0:
                            pe.wait_ge(*q3_ready(g3, PAIRS))
                            pe.wait_ge(*k3_ready(g3, PAIRS))
                            pe.wait_ge(*v3_ready(g3, GB))
                        tile = ("S3", b)
                        if emptied(turn, tile):
                            pe.wait_ge(*emptied(turn, tile))
                        o = psum[turn.bank(tile)]
                        for t in range(4):
                            for a in range(2):
                                last = mm(o[64 * a:64 * a + 64, t * P:(t + 1) * P], Q3[:, 2 * t + a, b, :],
                                          K3[:, 2 * t + a, b, :, :].rearrange("p g k -> p (g k)"), start=(t == 0))
                        fill(turn, tile, last)

                    def values3(b):
                        tile = ("O3", b)
                        if emptied(turn, tile):
                            pe.wait_ge(*emptied(turn, tile))
                        o = psum[turn.bank(tile)]
                        for t in (3, 2, 1, 0):
                            mm(o[:, 64 * (3 + t):64 * (5 + t)], V3[:, b, 2 * t + 1].rearrange("p g d -> p (g d)"),
                               softmax3.probT[:, b % NSLOT_T, t, :])
                        for t in range(4):
                            n = P if t < 3 else L
                            last = mm(o[:, 64 * t:64 * t + n], V3[:, b, 2 * t].rearrange("p g d -> p (g d)"),
                                      softmax3.probT[:, b % NSLOT_T, t, 0:n])
                        fill(turn, tile, last)

                    attention(turn, g3, s, softmax3, 0, ("S3",), ("PT3",), scores3, values3)
                elif kind == "out3":
                    k = step[1]
                    if k == 0:
                        pe.wait_ge(*ctx3_ready(turn.finish, GB))
                        pe.wait_ge(*emptied(turn, "y3"))
                    o = psum[turn.bank("y3")]
                    for p in range(PAIRS):
                        last = mm(o[:, k * P:(k + 1) * P],
                                  Q3[:, p, 2 * k:2 * k + 2, :].rearrange("p b q -> p (b q)"),
                                  w("wo3", p * P), start=(p == 0), stop=(p == PAIRS - 1))
                    if k == CH - 1:
                        fill(turn, "y3", last)

            run(pe, steps)

        @block.scalar
        def _(act):
            def split(columns, done):
                nc.scalar.activation(w_high[:, columns], w_stage[:, columns], ACT.Identity).then_inc(done, 1)

            def steps(turn, step):
                kind, g = step[0], turn.chain
                if kind == "load":
                    act.wait_ge(*filled(turn, "cT"))
                    o = psum[turn.bank("cT")]
                    nc.scalar.activation(c_high[:, 0:TOK], o[:, :], ACT.Identity)
                    nc.scalar.activation(c_high[:, TOK:TOK + L], o[:, 0:L], ACT.Identity)\
                        .then_inc(c_high_ready.sem, 1)
                elif kind == "q":
                    l = step[1]
                    if turn.phase == "first" and l == 0:
                        act.wait_ge(split_first_loaded, 16)
                        split(slice(0, FIRST_SPLIT), high_first)
                        act.wait_ge(constants_done, 2)
                    act.wait_ge(*filled(turn, step))
                    o = psum[turn.bank(step)]
                    for k in range(4):
                        last = nc.scalar.activation(Qm[:, :, k, :], o[:, :].rearrange("p (b q) -> p b q", b=GB),
                                                    ACT.Identity, bias=bqm[:, l, k:k + 1], scale=c("m_sa", k))
                    last.then_inc(qm_ready.sem, 1)
                    if turn.phase == "first" and l == 0:
                        act.wait_ge(split_rest_loaded, 16)
                        split(slice(FIRST_SPLIT, SPLIT_COLS), high_rest)
                elif kind in ("att", "att3"):
                    three = kind == "att3"
                    s = step[-1]
                    sm, grp, n0 = (softmax3, turn.finish, 0) if three else (softmax01, g, GB * step[1])
                    S_, PT_ = (("S3",), ("PT3",)) if three else (("S", step[1]), ("PT", step[1]))
                    if 0 <= s - 1 < GB:
                        b = s - 1
                        act.wait_ge(*sm.shifted(grp, n0 + b + 1))
                        if three and b == 0:
                            act.wait_ge(*rms_rows_ready(grp, 1))
                        o = psum[turn.bank((*S_, b))]
                        nc.scalar.activation(sm.prob[:, b % NSLOT].rearrange("p c k -> p (c k)"), o[:, :], ACT.Exp,
                                             scale=rms_rows[:, b:b + 1] if three else SCALE8).then_inc(sm.exp_ready.sem, 1)
                    if 0 <= s - 3 < GB:
                        b = s - 3
                        tile = (*PT_, b)
                        act.wait_ge(*filled(turn, tile))
                        if not three and n0 + b >= NSLOT_T:
                            act.wait_ge(*pv_done(grp, n0 + b + 1 - NSLOT_T))
                        o = psum[turn.bank(tile)]
                        nc.scalar.activation(sm.probT[:, b % NSLOT_T].rearrange("p t q -> p (t q)"), o[:, :],
                                             ACT.Identity).then_inc(sm.probT_ready.sem, 1)
                    if three and s >= DEPTH:
                        b = s - DEPTH
                        tile = ("O3", b)
                        act.wait_ge(*filled(turn, tile))
                        o = psum[turn.bank(tile)]
                        nc.scalar.activation(
                            Q3[:, :, b, :].rearrange("p (t a) q -> p a t q", a=2),
                            o[:, :].rearrange("p (a t q) -> p a t q", a=2, t=4), ACT.Identity
                        ).then_inc(ctx3_ready.sem, 1)
                elif kind == "lnF":
                    n = step[1]
                    if n < 2:
                        act.wait_ge(*filled(turn, step))
                        o = psum[turn.bank(step)]
                        dst = (x1T, x2T)[n]
                        nc.scalar.activation(dst[:, :], o[:, :], ACT.Identity, bias=v(f"ln{n + 1}_b"),
                                             scale=v(f"ln{n + 1}_g")).then_inc(ln_out.sem, 1)
                    else:
                        act.wait_ge(*yn_ready(g, 1))
                        nc.scalar.activation(yn_high[:, :], x2T[:, :], ACT.Identity).then_inc(yn_high_ready.sem, 1)
                elif kind == "rms":
                    act.wait_ge(*y_ready(turn.finish, 1))
                    for k in range(CH):
                        last = nc.scalar.activation(z[:, k, :], y[:, k, :], ACT.Square, scale=P ** -0.5,
                                                    accum_out=msum[:, k:k + 1])
                    last.then_inc(square_done.sem, 1)
                elif kind == "ffn":
                    l = step[1]
                    for j in range(FT):
                        tile = ("h", l, j)
                        act.wait_ge(*filled(turn, tile))
                        o = psum[turn.bank(tile)]
                        nc.scalar.activation(hT[:, j, :], o[:, :], ACT.Relu if l == 0 else ACT.Gelu_apprx_tanh,
                                             bias=v(f"b1_{l}_{j}")).then_inc(h_ready.sem, 1)
                    if l == 1:
                        nc.scalar.activation(table_scratch[:, :], half[:, 0:1], ACT.Exp)
                elif kind == "tp":
                    act.wait_ge(*filled(turn, "tp"))
                    o = psum[turn.bank("tp")]
                    nc.scalar.activation(tpT[:, :], o[:, :], ACT.Identity, bias=v("bt")).then_inc(tp_ready.sem, 1)
                elif kind == "gate" and step[1] == 0:
                    act.wait_ge(*centred(g, 1))
                    nc.scalar.activation(route[:, :], agree_in[:, :], ACT.Exp, scale=2.0)\
                        .then_inc(agree_exp.sem, 1)
                elif kind == "gate" and step[1] == 1:
                    act.wait_ge(*gate_b(g, 1))
                    nc.scalar.activation(gate[:, :], tpT[:, :], ACT.Tanh, bias=bg_half[:, 0:1], scale=0.5)\
                        .then_inc(gate_ready.sem, 1)
                elif kind == "q3":
                    p = step[1]
                    act.wait_ge(*filled(turn, step))
                    o = psum[turn.bank(step)]
                    last = nc.scalar.activation(Q3[:, p].rearrange("p b q -> p (b q)"), o[:, :], ACT.Identity)
                    last.then_inc(q3_ready.sem, 1)
                elif kind == "k3":
                    p = step[1]
                    act.wait_ge(*filled(turn, step))
                    if turn.phase == "first" and p == 0:
                        act.wait_ge(keys_cleared, 2)
                        act.wait_ge(values_cleared, 1)
                    o = psum[turn.bank(step)]
                    for c2 in range(2):
                        h = slice(64 * c2, 64 * c2 + 64)
                        own = (slice(0, 4, 3), slice(1, 3))[c2]
                        last = nc.scalar.activation(
                            K3[h, p].rearrange("d (m e) g k -> d m (e g) k", e=2)[:, :, own, :],
                            o[h, :].rearrange("d (m e k) -> d m e k", e=2, k=L), ACT.Identity)
                    last.then_inc(k3_ready.sem, 1)
                elif kind == "v3":
                    b = step[1]
                    act.wait_ge(*filled(turn, step))
                    o = psum[turn.bank(step)]
                    for half_of in range(2):
                        h = slice(64 * half_of, 64 * half_of + 64)
                        last = nc.scalar.activation(V3[h, (b + half_of) % GB, :, b % 2, :],
                                                    o[h, :].rearrange("k (p d) -> k p d", p=PAIRS), ACT.Identity)
                    last.then_inc(v3_ready.sem, 1)

            run(act, steps)

        @block.gpsimd
        def _(pool):
            pool.memset(half[:, :], -0.5)
            pool.memset(ln_eps[:, :], LN_EPS)
            pool.memset(rms_eps[:, :], RMS_EPS)
            pool.memset(ones[:, :], 1.0).then_inc(constants_done, 1)
            pool.memset(V3[:, :, :, :, :], 0.0).then_inc(values_cleared, 1)
            pool.memset(K3[:, PAIRS // 2:, :, :, :], 0.0).then_inc(keys_cleared, 1)
            pool.wait_ge(high_rest, 1)
            rest = slice(FIRST_SPLIT, SPLIT_COLS)
            nc.gpsimd.tensor_tensor(w_low[:, rest], w_stage[:, rest], w_high[:, rest], ALU.subtract)\
                .then_inc(low_rest, 1)

            def steps(turn, step):
                kind, g = step[0], turn.chain
                if kind in ("att", "att3"):
                    three = kind == "att3"
                    s = step[-1]
                    sm, grp, n0 = (softmax3, turn.finish, 0) if three else (softmax01, g, GB * step[1])
                    b = s - 1 if three else s - 2
                    if 0 <= b < GB:
                        pool.wait_ge(*sm.rinv_ready(grp, n0 + b + 1))
                        pr = sm.prob[:, b % NSLOT]
                        ri = sm.rinv[:, b % NSLOT, :].unsqueeze(2).broadcast_to([P, 8, L])
                        nc.gpsimd.tensor_tensor(pr, pr, ri, ALU.mult).then_inc(sm.norm_ready.sem, 1)
                elif kind == "lnT":
                    n = step[1]
                    pool.wait_ge(*mv_ready(g, n + 1))
                    nc.gpsimd.tensor_tensor(var_eps[:, :], mv[:, :, 1], ln_eps[:, :], ALU.add)\
                        .then_inc(var_ready.sem, 1)
                    pool.wait_ge(*var_ready(g, n + 1))
                    nc.gpsimd.tensor_tensor(rstd[:, :], var_eps[:, :], half[:, :], ALU.pow)\
                        .then_inc(rstd_ready.sem, 1)
                elif kind == "rms":
                    pool.wait_ge(*square_done(turn.finish, 1))
                    nc.gpsimd.tensor_tensor(ms_eps[:, :], msum[:, :], rms_eps[:, :], ALU.add)\
                        .then_inc(ms_ready.sem, 1)
                    pool.wait_ge(*ms_ready(turn.finish, 1))
                    nc.gpsimd.tensor_tensor(rms[:, :], ms_eps[:, :], half[:, :], ALU.pow)\
                        .then_inc(rms_ready.sem, 1)

            run(pool, steps)

        @block.vector
        def _(dve):
            dve.memset(K3[:, 0:PAIRS // 2, :, :, :], 0.0).then_inc(keys_cleared, 1)
            dve.wait_ge(constants_loaded, 16 * 2)
            dve.tensor_copy(ident_b[:, :], ident)
            dve.tensor_copy(causal_b[:, :], c("causal", 0, L))
            for l in range(2):
                dve.tensor_scalar(bqm[:, l, :], c("m_sa", 0, 4), v(f"bq{l}"), None, ALU.mult)
            dve.tensor_scalar(yn_scale[:, :], vec[:, VEC["gamma"]:VEC["gamma"] + 2], v("norm_w"), None, ALU.mult)
            dve.tensor_scalar(bg_half[:, :], v("bg"), 0.5, None, ALU.mult).then_inc(constants_done, 1)

            def seqs(ap):
                return ap.rearrange("p (b q) -> p b q", b=GB)

            def over_tokens(ap):
                return ap[:, :].unsqueeze(2).broadcast_to([P, GB, L])

            def steps(turn, step):
                kind, g = step[0], turn.chain
                if kind == "load":
                    dve.wait_ge(*filled(turn, "xT"))
                    nc.vector.tensor_copy(xT[:, :], psum[turn.bank("xT")][:, :]).then_inc(xT_ready.sem, 1)
                    dve.wait_ge(*c_high_ready(g, 1))
                    o = psum[turn.bank("cT")]
                    nc.vector.tensor_tensor(c_low[:, 0:TOK], o[:, :], c_high[:, 0:TOK], ALU.subtract)
                    nc.vector.tensor_tensor(c_low[:, TOK:TOK + L], o[:, 0:L], c_high[:, TOK:TOK + L], ALU.subtract)\
                        .then_inc(c_low_ready.sem, 1)
                    nc.vector.tensor_copy(cT[:, :], o[:, :]).then_inc(cT_ready.sem, 1)
                    if turn.phase == "first":
                        dve.wait_ge(high_first, 1)
                        first = slice(0, FIRST_SPLIT)
                        nc.vector.tensor_tensor(w_low[:, first], w_stage[:, first], w_high[:, first], ALU.subtract)\
                            .then_inc(low_first, 1)
                elif kind == "k":
                    l = step[1]
                    dve.wait_ge(*filled(turn, step))
                    o = psum[turn.bank(step)]
                    for k in range(4):
                        last = nc.vector.tensor_scalar(Km[:, :, k, :], seqs(o[:, :]), v(f"bk{l}"), c("m_c", k),
                                                       ALU.add, ALU.mult)
                    last.then_inc(km_ready.sem, 1)
                elif kind == "v":
                    l = step[1]
                    for hf in range(2):
                        dve.wait_ge(*filled(turn, ("v", l, hf)))
                        o = psum[turn.bank(("v", l, hf))]
                        last = nc.vector.tensor_tensor(
                            Vm[:, 4 * hf:4 * hf + 4, :], o[:, :].rearrange("p (b f) -> p b f", b=4),
                            c("m_v", 0, P).unsqueeze(1).broadcast_to([P, 4, P]), ALU.mult)
                        last.then_inc(vm_ready.sem, 1)
                elif kind in ("att", "att3"):
                    three = kind == "att3"
                    s = step[-1]
                    sm, grp, n0 = (softmax3, turn.finish, 0) if three else (softmax01, g, GB * step[1])
                    if s < GB:
                        b = s
                        tile = ("S3", b) if three else ("S", step[1], b)
                        dve.wait_ge(*filled(turn, tile))
                        o = psum[turn.bank(tile)]
                        nc.vector.tensor_reduce(sm.negmax[:, b % NSLOT, :], o[:, :].rearrange("p (c k) -> p c k", c=8),
                                                AX.X, ALU.max, negate=True).then_inc(sm.max_ready.sem, 1)
                    if 0 <= s - 1 < GB:
                        b = s - 1
                        dve.wait_ge(*sm.exp_ready(grp, n0 + b + 1))
                        nc.vector.tensor_reduce(sm.sums[:, b % NSLOT, :], sm.prob[:, b % NSLOT], AX.X, ALU.add)\
                            .then_inc(sm.sum_ready.sem, 1)
                        dve.wait_ge(*sm.sum_ready(grp, n0 + b + 1))
                        if n0 + b >= NSLOT:
                            dve.wait_ge(*sm.norm_ready(grp, n0 + b + 1 - NSLOT))
                        nc.vector.reciprocal(sm.rinv[:, b % NSLOT, :], sm.sums[:, b % NSLOT, :])\
                            .then_inc(sm.rinv_ready.sem, 1)
                    if not three and s >= DEPTH and (s - DEPTH) % 4 == 3:
                        l, hf = step[1], (s - DEPTH) // 4
                        dve.wait_ge(*pv_done(g, n0 + 4 * hf + 4))
                        o = psum[turn.bank(("O", l, hf))][:, :].rearrange("p (b a q) -> p a b q", b=4, a=2)
                        q0 = 1 if l == 0 else 0
                        if l == 0:
                            nc.vector.memset(aT[:, 4 * hf:4 * hf + 4, 0:1], 0.0)
                        nc.vector.tensor_scalar(half_ctx[:, hf, :, q0:L], o[:, 0, :, q0:L], c("m_a", 0), v(f"bv{l}"),
                                                ALU.mult, ALU.add).then_inc(half_ready.sem, 1)
                        dve.wait_ge(*half_ready(g, 2 * l + hf + 1))
                        last = nc.vector.scalar_tensor_tensor(aT[:, 4 * hf:4 * hf + 4, q0:L], o[:, 1, :, q0:L],
                                                              c("m_a", 1), half_ctx[:, hf, :, q0:L], ALU.mult, ALU.add)
                        last.then_inc(ctx_half.sem, 1)
                elif kind == "attout":
                    l = step[1]
                    dve.wait_ge(*filled(turn, ("o", l)))
                    o = psum[turn.bank(("o", l))]
                    nc.vector.scalar_tensor_tensor(fT[:, :], o[:, :], v(f"bo{l}"), (xT if l == 0 else x2T)[:, :],
                                                   ALU.add, ALU.add).then_inc(f_ready.sem, 1)
                elif kind == "lnT":
                    n = step[1]
                    dve.wait_ge(*filled(turn, step))
                    o = psum[turn.bank(step)]
                    for k in range(CH):
                        last = nc.vector.bn_stats(stats[:, k, :], o[:, k * P:(k + 1) * P])
                    last.then_inc(stats_ready.sem, 1)
                    dve.wait_ge(*stats_ready(g, n + 1))
                    nc.vector.tensor_copy(stats_wait[:, :], stats[:, 0, 0:1])
                    for k in range(CH):
                        last = nc.vector.bn_aggr(mv[:, k, :], stats[:, k, :])
                    last.then_inc(mv_ready.sem, 1)
                    dve.wait_ge(*mv_ready(g, n + 1))
                    for k in range(CH):
                        last = nc.vector.tensor_scalar(z[:, k, :], o[:, k * P:(k + 1) * P], mv[:, k, 0:1],
                                                       None, ALU.subtract)
                    last.then_inc(ln_centred.sem, 1)
                elif kind == "lnZ":
                    n = step[1]
                    dve.wait_ge(*ln_centred(g, n + 1))
                    dve.wait_ge(*rstd_ready(g, n + 1))
                    nc.vector.tensor_tensor(z[:, :, :], z[:, :, :], rstd[:, :].unsqueeze(2).broadcast_to([P, CH, P]),
                                            ALU.mult).then_inc(z_ready.sem, 1)
                    if n == 2:
                        if turn.phase == "first":
                            dve.wait_ge(rest_loaded, 16 * 2)
                        dve.wait_ge(*z_ready(g, 3))
                        dve.wait_ge(*y_free(g, 16))
                        nc.vector.tensor_tensor(y[:, :, :], z[:, :, :],
                                                gamma[:, :].unsqueeze(1).broadcast_to([P, CH, P]), ALU.mult)\
                            .then_inc(y_a.sem, 1)
                elif kind == "rms":
                    dve.wait_ge(*yn_high_ready(turn.finish, 1))
                    nc.vector.tensor_tensor(yn_low[:, :], x2T[:, :], yn_high[:, :], ALU.subtract)\
                        .then_inc(yn_low_ready.sem, 1)
                    dve.wait_ge(*y_a(turn.finish, 1))
                    nc.vector.tensor_tensor(y[:, :, :], y[:, :, :],
                                            beta[:, :].unsqueeze(1).broadcast_to([P, CH, P]), ALU.add)\
                        .then_inc(y_ready.sem, 1)
                elif kind == "rms_rows":
                    g3 = turn.finish
                    dve.wait_ge(*rms_ready(g3, 1))
                    own = cst[:, CCOL["m_v"]:CCOL["m_v"] + 16].rearrange("p (e f) -> p e f", e=2)[:, :, 0]
                    nc.vector.tensor_tensor(rms_own[:, :, :], rms[:, :].unsqueeze(2).broadcast_to([P, CH, 2]),
                                            own.unsqueeze(1).broadcast_to([P, CH, 2]), ALU.mult)\
                        .then_inc(rms_own_ready.sem, 1)
                    dve.wait_ge(*filled(turn, "rms_rows"))
                    o = psum[turn.bank("rms_rows")]
                    nc.vector.tensor_copy(rms_rows[:, :], o[:, 0:GB]).then_inc(rms_rows_ready.sem, 1)
                elif kind == "lnF" and step[1] == 2:
                    dve.wait_ge(*filled(turn, step))
                    o = psum[turn.bank(step)]
                    nc.vector.tensor_scalar(x2T[:, :], o[:, :], yn_scale[:, 0:1], yn_scale[:, 1:2],
                                            ALU.mult, ALU.add).then_inc(yn_ready.sem, 1)
                elif kind == "ffn":
                    l = step[1]
                    dve.wait_ge(*filled(turn, ("f", l)))
                    o = psum[turn.bank(("f", l))]
                    if l == 0:
                        nc.vector.scalar_tensor_tensor(fT[:, :], o[:, :], v("b2_0"), x1T[:, :], ALU.add, ALU.add)\
                            .then_inc(f_ready.sem, 1)
                    else:
                        nc.vector.scalar_tensor_tensor(x1T[:, :], o[:, :], v("b2_1"), fT[:, :], ALU.add, ALU.add)\
                            .then_inc(f_ready.sem, 1)
                elif kind == "pool":
                    dve.wait_ge(*cT_ready(g, 1))
                    nc.vector.tensor_reduce(pooled[:, :], seqs(cT[:, :]), AX.X, ALU.add)\
                        .then_inc(pooled_ready.sem, 1)
                elif kind == "vis":
                    dve.wait_ge(*filled(turn, "vis"))
                    o = psum[turn.bank("vis")]
                    nc.vector.tensor_scalar(vis[:, :], o[:, 0:GB], 1.0 / L, v("bvis"), ALU.mult, ALU.add)\
                        .then_inc(vis_ready.sem, 1)
                elif kind == "gv":
                    dve.wait_ge(*filled(turn, "gv"))
                    o = psum[turn.bank("gv")]
                    nc.vector.tensor_copy(gv[:, :], o[:, 0:GB]).then_inc(gv_ready.sem, 1)
                elif kind == "agree":
                    dve.wait_ge(*tp_ready(g, 1))
                    dve.wait_ge(*vis_ready(g, 1))
                    nc.vector.tensor_tensor(seqs(agree_in[:, :]), seqs(tpT[:, :]), over_tokens(vis), ALU.mult)\
                        .then_inc(agree_in_ready.sem, 1)
                elif kind == "gate" and step[1] == 0:
                    dve.wait_ge(*filled(turn, "ag"))
                    o = psum[turn.bank("ag")]
                    nc.vector.tensor_reduce(amax[:, :], seqs(o[:, :]), AX.X, ALU.max).then_inc(amax_ready.sem, 1)
                    dve.wait_ge(*amax_ready(g, 1))
                    nc.vector.tensor_tensor(seqs(agree_in[:, :]), seqs(o[:, :]), over_tokens(amax), ALU.subtract)\
                        .then_inc(centred.sem, 1)
                elif kind == "gate" and step[1] == 1:
                    dve.wait_ge(*agree_exp(g, 1))
                    nc.vector.tensor_reduce(asum[:, :], seqs(route[:, :]), AX.X, ALU.add).then_inc(asum_ready.sem, 1)
                    dve.wait_ge(*asum_ready(g, 1))
                    nc.vector.reciprocal(ainv[:, :], asum[:, :]).then_inc(ainv_ready.sem, 1)
                    dve.wait_ge(*ainv_ready(g, 1))
                    dve.wait_ge(*gv_ready(g, 1))
                    nc.vector.tensor_tensor(gv_route[:, :], gv[:, :], ainv[:, :], ALU.mult)\
                        .then_inc(gv_route_ready.sem, 1)
                    nc.vector.tensor_tensor(vis_route[:, :], vis[:, :], ainv[:, :], ALU.mult)\
                        .then_inc(vis_route_ready.sem, 1)
                    dve.wait_ge(*gv_route_ready(g, 1))
                    nc.vector.tensor_tensor(seqs(fT[:, :]), seqs(route[:, :]), over_tokens(gv_route), ALU.mult)\
                        .then_inc(gate_a.sem, 1)
                    dve.wait_ge(*gate_a(g, 1))
                    dve.wait_ge(*filled(turn, "gp"))
                    o = psum[turn.bank("gp")]
                    nc.vector.tensor_tensor(tpT[:, :], o[:, :], fT[:, :], ALU.add).then_inc(gate_b.sem, 1)
                    dve.wait_ge(*vis_route_ready(g, 1))
                    nc.vector.tensor_tensor(seqs(route[:, :]), seqs(route[:, :]), over_tokens(vis_route), ALU.mult)\
                        .then_inc(route_ready.sem, 1)
                elif kind == "gate" and step[1] == 2:
                    dve.wait_ge(*gate_ready(g, 1))
                    dve.wait_ge(*route_ready(g, 1))
                    nc.vector.scalar_tensor_tensor(gate[:, :], gate[:, :], 1.0, route[:, :], ALU.add, ALU.mult)\
                        .then_inc(gate_c.sem, 1)
                    dve.wait_ge(*gate_c(g, 1))
                    nc.vector.scalar_tensor_tensor(fT[:, :], gate[:, :], 0.5, x1T[:, :], ALU.mult, ALU.add)\
                        .then_inc(f_ready.sem, 1)
                elif kind == "out3" and step[1] == CH - 1:
                    dve.wait_ge(*filled(turn, "y3"))
                    o = psum[turn.bank("y3")]
                    nc.vector.tensor_tensor(y[:, :, :], o[:, :].rearrange("p (c f) -> p c f", c=CH),
                                            y[:, :, :], ALU.add).then_inc(out_ready.sem, 1)

            run(dve, steps)


def kernel(**inputs):
    import numpy as np
    import concourse.bacc as bacc
    from concourse.bass_utils import run_bass_kernel_spmd

    a = {k: np.asarray(val) for k, val in inputs.items()}
    l0, l1, l2, l3 = (lambda n: a["L0_xattn_" + n]), (lambda n: a["L1_xattn_" + n]), \
        (lambda n: a["L2_xattn_" + n]), (lambda n: a["L3_xattn_" + n])

    def rows_to_columns(m):
        n = m.shape[0] // P
        return m.reshape(n, P, m.shape[1]).transpose(1, 0, 2).reshape(P, -1)

    mats = {"Wq0": l0("Wq"), "Wk0": l0("Wk"), "Wv0": l0("Wv"), "Wo0": l0("Wo"),
            "Wq1": l1("Wq"), "Wk1": l1("Wk"), "Wv1": l1("Wv"), "Wo1": l1("Wo"),
            "WtT": l2("Wt").T, "WvisT": l2("Wv").T, "WgtT": l2("Wg")[:, :P].T, "WgvT": l2("Wg")[:, P:].T,
            "W1_0": l0("W1"), "W2_0": rows_to_columns(l0("W2")), "W1_1": l1("W1"), "W2_1": rows_to_columns(l1("W2")),
            "wq3": l3("wq"), "wk3": l3("wk"),
            "wv3": l3("wv").reshape(P, PAIRS, 2, L).transpose(0, 2, 1, 3).reshape(P, -1),
            "wo3": rows_to_columns(l3("wo"))}
    weights = np.ascontiguousarray(np.concatenate([mats[n] for n in WCOL], axis=1))
    split_weights = np.ascontiguousarray(np.concatenate([mats[n] for n in SPLIT], axis=1))
    vecs = {"bq0": l0("bq"), "bk0": l0("bk"), "bv0": l0("bv"), "bo0": l0("bo"), "ln1_g": l0("ln1_g"),
            "ln1_b": l0("ln1_b"), "b2_0": l0("b2"), "ln2_g": l0("ln2_g"), "ln2_b": l0("ln2_b"),
            "bq1": l1("bq"), "bk1": l1("bk"), "bv1": l1("bv"), "bo1": l1("bo"), "b2_1": l1("b2"),
            "bt": l2("bt"), "bvis": l2("bv"), "bg": l2("bg"), "gamma": l2("gamma"), "beta": l2("beta"),
            "norm_w": l3("norm_w")}
    for l, b1 in enumerate((l0("b1"), l1("b1"))):
        for j in range(FT):
            vecs[f"b1_{l}_{j}"] = b1[j * P:(j + 1) * P]
    vectors = np.ascontiguousarray(np.stack([vecs[n] for n in VEC], axis=1))

    f = np.arange(P)
    t, am, c2 = f // 32, (f // 16) % 2, (f // 8) % 2
    q, k = np.arange(P)[:, None] % L, np.arange(L)[None, :]
    constants = np.zeros((P, CCOLS), np.float32)
    constants[:, 0:P] = np.eye(P)
    constants[:, CCOL["causal"]:CCOL["causal"] + L] = np.where((k < q) | (q == 0), 0.0, -1e30)
    for i in range(4):
        constants[:, CCOL["m_sa"] + i] = (t // 2 == i // 2) & (am == i % 2)
        constants[:, CCOL["m_c"] + i] = (t % 2 == i // 2) & (c2 == i % 2)
    for i in range(2):
        constants[:, CCOL["m_a"] + i] = am == i
    constants[:, CCOL["m_v"]:CCOL["m_v"] + P] = c2[None, :] == (np.arange(P) // L)[:, None]

    constants[:, CCOL["rows"]:CCOL["rows"] + P] = q == np.arange(P)[None, :] % L

    arrays = {"x": np.ascontiguousarray(a["x"]).reshape(B * L, P),
              "ctx": np.ascontiguousarray(a["ctx_1024"]).reshape(B * L, P),
              "weights": weights, "split_weights": split_weights, "vectors": vectors,
              "gamma": np.ascontiguousarray(np.broadcast_to(l2("gamma"), (P, P))),
              "beta": np.ascontiguousarray(np.broadcast_to(l2("beta"), (P, P))),
              "constants": constants}
    nc = bacc.Bacc("TRN2", target_bir_lowering=False, num_devices=1)
    args = [nc.dram_tensor("in_" + n, m.shape, mybir.dt.from_np(m.dtype), kind="ExternalInput").ap()
            for n, m in arrays.items()]
    args.append(nc.dram_tensor("out", (B * L, P), F32, kind="ExternalOutput").ap())
    xattn_sequence_kernel(nc, *args)
    r = run_bass_kernel_spmd(nc, [{"in_" + n: m for n, m in arrays.items()}], core_ids=[0])
    return r.results[0]["out"].reshape(B, L, P)
```
